# Optimizing a Trainium2 kernel written in Bass

```python
import numpy as np
import jax
import jax.numpy as jnp

def _softmax(x, axis=-1):
    return jax.nn.softmax(x, axis=axis)

def _gelu(x):
    return jax.nn.gelu(x, approximate=True)

def _silu(x):
    return jax.nn.silu(x)

def _sigmoid(x):
    return jax.nn.sigmoid(x)

def _layernorm(x, axis=-1, eps=1e-05):
    m = jnp.mean(x, axis=axis, keepdims=True)
    v = jnp.var(x, axis=axis, keepdims=True)
    return (x - m) / jnp.sqrt(v + eps)

def _scatter_add(tgt, idx, src, axis=0):
    return tgt.at[idx].add(src)

def _segment_sum(src, seg, n):
    return jax.ops.segment_sum(src, seg, n)
kernel_name = 'mk_vit_tower_postln_d4_tok_img1024_r4_c03c64'

def setup_inputs(seed: int=0):
    np.random.seed(seed)
    _w = jnp.asarray

    def _rec_inputs():
        import jax
        import jax.numpy as jnp
        _rk = jax.random.key(seed)
        x = -0.000222058 + 0.999998 * jax.random.normal(jax.random.fold_in(_rk, 1), (32, 3, 128, 128), jnp.float32)
        return x
    x = _rec_inputs()

    def _L0_tok_setup():
        import jax, jax.numpy as jnp
        import numpy as np
        P = 16
        key = jax.random.key(seed)
        kx, kw, kb = jax.random.split(key, 3)
        B, C, H, W_ = (32, 3, 128, 128)
        in_dim, embed_dim = (C * P * P, 256)
        x = jax.random.normal(kx, (B, C, H, W_), dtype=jnp.float32)
        bound = 1.0 / np.sqrt(in_dim)
        W = jax.random.uniform(kw, (embed_dim, in_dim), minval=-bound, maxval=bound, dtype=jnp.float32)
        b = jax.random.uniform(kb, (embed_dim,), minval=-bound, maxval=bound, dtype=jnp.float32)
        return {'x': x, 'W': W, 'b': b}
    _L0_tok_all = _L0_tok_setup()
    _L0_tok_in = {k: v for k, v in _L0_tok_all.items() if k in ('W', 'b')}
    del _L0_tok_all

    def _L0_attn_setup():
        import jax, jax.numpy as jnp
        import numpy as np
        DIM = 256
        H = 16
        D = DIM // H
        SCALE = D ** (-0.5)
        EPS = 1e-05

        def _layernorm(x, w, b):
            xf = x.astype(jnp.float32)
            mu = xf.mean(-1, keepdims=True)
            var = xf.var(-1, keepdims=True)
            y = (xf - mu) / jnp.sqrt(var + EPS) * w.astype(jnp.float32) + b.astype(jnp.float32)
            return y.astype(x.dtype)
        key = jax.random.key(seed)
        ks = jax.random.split(key, 8)
        x = jax.random.normal(ks[0], (2, 512, DIM), dtype=jnp.float32)
        qkv_w = jax.random.normal(ks[1], (3 * DIM, DIM), dtype=jnp.float32) * DIM ** (-0.5)
        q_norm_w = jnp.ones((D,), jnp.float32)
        q_norm_b = jnp.zeros((D,), jnp.float32)
        k_norm_w = jnp.ones((D,), jnp.float32)
        k_norm_b = jnp.zeros((D,), jnp.float32)
        proj_w = jax.random.normal(ks[2], (DIM, DIM), dtype=jnp.float32) * DIM ** (-0.5)
        proj_b = jnp.zeros((DIM,), jnp.float32)
        return {'x': x, 'qkv_w': qkv_w, 'q_norm_w': q_norm_w, 'q_norm_b': q_norm_b, 'k_norm_w': k_norm_w, 'k_norm_b': k_norm_b, 'proj_w': proj_w, 'proj_b': proj_b}
    _L0_attn_all = _L0_attn_setup()
    _L0_attn_in = {k: v for k, v in _L0_attn_all.items() if k in ('qkv_w', 'q_norm_w', 'q_norm_b', 'k_norm_w', 'k_norm_b', 'proj_w', 'proj_b')}
    del _L0_attn_all

    def _L0_ffn_setup():
        import jax, jax.numpy as jnp
        import numpy as np
        EPS = 1e-06
        TOP_K = 2

        def rms_norm(x, scale, eps=EPS):
            xf = x.astype(jnp.float32)
            mean_sq = jnp.mean(xf * xf, axis=-1, keepdims=True)
            return (xf * (scale.astype(jnp.float32) * jax.lax.rsqrt(mean_sq + eps))).astype(x.dtype)
        key = jax.random.key(seed)
        k0, k1, k2, k3 = jax.random.split(key, 4)
        B, S, D, H, E = (2, 512, 256, 704, 8)
        x = jax.random.normal(k0, (B, S, D), dtype=jnp.float32)
        norm_scale = jnp.ones((D,), dtype=jnp.float32)
        w_router = jax.random.normal(k1, (E, D), dtype=jnp.float32) * 0.02
        w_up = jax.random.normal(k2, (E, 2 * H, D), dtype=jnp.float32) * 0.02
        w_down = jax.random.normal(k3, (E, D, H), dtype=jnp.float32) * 0.02
        return {'x': x, 'norm_scale': norm_scale, 'w_router': w_router, 'w_up': w_up, 'w_down': w_down}
    _L0_ffn_all = _L0_ffn_setup()
    _L0_ffn_in = {k: v for k, v in _L0_ffn_all.items() if k in ('norm_scale', 'w_router', 'w_up', 'w_down')}
    del _L0_ffn_all

    def _L1_attn_setup():
        import jax, jax.numpy as jnp
        import numpy as np
        EPS = 1e-06
        key = jax.random.key(seed)
        ks = jax.random.split(key, 8)
        b, n, d, h = (2, 512, 256, 16)
        std = 0.02
        x = jax.random.normal(ks[0], (b, n, d), jnp.float32)
        Wq = jax.random.normal(ks[1], (d, d), jnp.float32) * std
        Wk = jax.random.normal(ks[2], (d, d), jnp.float32) * std
        Wv = jax.random.normal(ks[3], (d, d), jnp.float32) * std
        Wo = jax.random.normal(ks[4], (d, d), jnp.float32) * std
        Wbet = jax.random.normal(ks[5], (d, h), jnp.float32) * std
        Wf = jax.random.normal(ks[6], (d, h), jnp.float32) * std
        norm_w = jnp.ones((d,), jnp.float32)
        return {'x': x, 'Wq': Wq, 'Wk': Wk, 'Wv': Wv, 'Wo': Wo, 'Wbet': Wbet, 'Wf': Wf, 'norm_w': norm_w}
    _L1_attn_all = _L1_attn_setup()
    _L1_attn_in = {k: v for k, v in _L1_attn_all.items() if k in ('Wq', 'Wk', 'Wv', 'Wo', 'Wbet', 'Wf', 'norm_w')}
    del _L1_attn_all

    def _L1_ffn_setup():
        import jax, jax.numpy as jnp
        import numpy as np
        DIM = 256

        def _reference_tuple_inner(x, W_r, W_k, W_v, mu_r, mu_k):
            B, T, C = x.shape
            x_prev = jnp.concatenate([jnp.zeros((B, 1, C), x.dtype), x[:, :-1, :]], axis=1)
            xr = mu_r * x + (1.0 - mu_r) * x_prev
            xk = mu_k * x + (1.0 - mu_k) * x_prev
            r = jax.nn.sigmoid(jnp.einsum('btc,dc->btd', xr, W_r))
            k = jnp.einsum('btc,dc->btd', xk, W_k)
            k_act = jnp.square(jax.nn.relu(k))
            out = r * jnp.einsum('btc,dc->btd', k_act, W_v)
            new_state = x[:, -1, :]
            return (out, new_state)
        key = jax.random.key(seed)
        ks = jax.random.split(key, 6)
        B, T, C = (8, 512, DIM)
        x = jax.random.normal(ks[0], (B, T, C), dtype=jnp.float32)
        s = 1.0 / np.sqrt(C)
        W_r = jax.random.uniform(ks[1], (C, C), jnp.float32, -s, s)
        W_k = jax.random.uniform(ks[2], (C, C), jnp.float32, -s, s)
        W_v = jax.random.uniform(ks[3], (C, C), jnp.float32, -s, s)
        mu_r = jax.random.uniform(ks[4], (C,), jnp.float32)
        mu_k = jax.random.uniform(ks[5], (C,), jnp.float32)
        return {'x': x, 'W_r': W_r, 'W_k': W_k, 'W_v': W_v, 'mu_r': mu_r, 'mu_k': mu_k}
    _L1_ffn_all = _L1_ffn_setup()
    _L1_ffn_in = {k: v for k, v in _L1_ffn_all.items() if k in ('W_r', 'W_k', 'W_v', 'mu_r', 'mu_k')}
    del _L1_ffn_all

    def _L2_attn_setup():
        import jax, jax.numpy as jnp
        import numpy as np
        import math
        D_MODEL = 256
        NUM_HEADS = 16
        HEAD_DIM = D_MODEL // NUM_HEADS
        key = jax.random.key(seed)
        k_x, k_qkv, k_o = jax.random.split(key, 3)
        B, S = (2, 512)
        x = jax.random.normal(k_x, (B, S, D_MODEL), dtype=jnp.float32)
        sigma_qkv = math.sqrt(2.0 / (D_MODEL + 3 * D_MODEL))
        w_qkv = jax.random.truncated_normal(k_qkv, -3.0, 3.0, (3 * D_MODEL, D_MODEL), dtype=jnp.float32) * sigma_qkv
        sigma_o = math.sqrt(2.0 / (D_MODEL + D_MODEL))
        w_out = jax.random.truncated_normal(k_o, -3.0, 3.0, (D_MODEL, D_MODEL), dtype=jnp.float32) * sigma_o
        return {'x': x, 'w_qkv': w_qkv, 'w_out': w_out}
    _L2_attn_all = _L2_attn_setup()
    _L2_attn_in = {k: v for k, v in _L2_attn_all.items() if k in ('w_qkv', 'w_out')}
    del _L2_attn_all

    def _L2_ffn_setup():
        import jax, jax.numpy as jnp
        import numpy as np
        DM, NE, ES, ESZ = (256, 16, 4, 64)
        BATCH, SEQ = (8, 512)
        key = jax.random.key(seed)
        k = jax.random.split(key, 5)
        scale = 0.02
        return {'x': jax.random.normal(k[0], (BATCH, SEQ, DM), dtype=jnp.float32), 'controller': jax.random.normal(k[1], (DM, NE, ES), dtype=jnp.float32) * scale, 'f1': jax.random.normal(k[2], (DM, NE, ES, ESZ), dtype=jnp.float32) * scale, 'f2': jax.random.normal(k[3], (NE, ES, ESZ, DM), dtype=jnp.float32) * scale, 'bias': jax.random.normal(k[4], (NE, ES, ESZ), dtype=jnp.float32) * scale}
    _L2_ffn_all = _L2_ffn_setup()
    _L2_ffn_in = {k: v for k, v in _L2_ffn_all.items() if k in ('controller', 'f1', 'f2', 'bias')}
    del _L2_ffn_all

    def _L3_attn_setup():
        import jax, jax.numpy as jnp
        import numpy as np
        B, K, D = (4, 2048, 256)
        key = jax.random.key(seed)
        kx, kw, kb = jax.random.split(key, 3)
        x = jax.random.normal(kx, (B, K, D), dtype=jnp.float32)
        bound = 1.0 / np.sqrt(D)
        W = jax.random.uniform(kw, (D, D), dtype=jnp.float32, minval=-bound, maxval=bound)
        b = jax.random.uniform(kb, (D,), dtype=jnp.float32, minval=-bound, maxval=bound)
        return {'x': x, 'W': W, 'b': b}
    _L3_attn_all = _L3_attn_setup()
    _L3_attn_in = {k: v for k, v in _L3_attn_all.items() if k in ('W', 'b')}
    del _L3_attn_all

    def _L3_ffn_setup():
        import jax, jax.numpy as jnp
        import numpy as np
        EPS = 1e-05
        key = jax.random.key(seed)
        kx, kw, kb = jax.random.split(key, 3)
        B, S, K, N = (8, 2048, 256, 256)
        x = jax.random.normal(kx, (B, S, K), dtype=jnp.float32)
        W = jax.random.normal(kw, (N, K), dtype=jnp.float32) * 0.02
        weight_scale = jnp.maximum(jnp.max(jnp.abs(W), axis=1, keepdims=True) / 127.0, EPS)
        weight_int8 = jnp.clip(jnp.round(W / weight_scale), -128, 127).astype(jnp.int8)
        bias = jax.random.normal(kb, (N,), dtype=jnp.float32) * 0.01
        return {'x': x, 'weight_int8': weight_int8, 'weight_scale': weight_scale, 'bias': bias}
    _L3_ffn_all = _L3_ffn_setup()
    _L3_ffn_in = {k: v for k, v in _L3_ffn_all.items() if k in ('weight_int8', 'weight_scale', 'bias')}
    del _L3_ffn_all
    return {'x': x, 'L0_tok_W': _L0_tok_in['W'], 'L0_tok_b': _L0_tok_in['b'], 'L0_attn_qkv_w': _L0_attn_in['qkv_w'], 'L0_attn_q_norm_w': _L0_attn_in['q_norm_w'], 'L0_attn_q_norm_b': _L0_attn_in['q_norm_b'], 'L0_attn_k_norm_w': _L0_attn_in['k_norm_w'], 'L0_attn_k_norm_b': _L0_attn_in['k_norm_b'], 'L0_attn_proj_w': _L0_attn_in['proj_w'], 'L0_attn_proj_b': _L0_attn_in['proj_b'], 'L0_ffn_norm_scale': _L0_ffn_in['norm_scale'], 'L0_ffn_w_router': _L0_ffn_in['w_router'], 'L0_ffn_w_up': _L0_ffn_in['w_up'], 'L0_ffn_w_down': _L0_ffn_in['w_down'], 'L1_attn_Wq': _L1_attn_in['Wq'], 'L1_attn_Wk': _L1_attn_in['Wk'], 'L1_attn_Wv': _L1_attn_in['Wv'], 'L1_attn_Wo': _L1_attn_in['Wo'], 'L1_attn_Wbet': _L1_attn_in['Wbet'], 'L1_attn_Wf': _L1_attn_in['Wf'], 'L1_attn_norm_w': _L1_attn_in['norm_w'], 'L1_ffn_W_r': _L1_ffn_in['W_r'], 'L1_ffn_W_k': _L1_ffn_in['W_k'], 'L1_ffn_W_v': _L1_ffn_in['W_v'], 'L1_ffn_mu_r': _L1_ffn_in['mu_r'], 'L1_ffn_mu_k': _L1_ffn_in['mu_k'], 'L2_attn_w_qkv': _L2_attn_in['w_qkv'], 'L2_attn_w_out': _L2_attn_in['w_out'], 'L2_ffn_controller': _L2_ffn_in['controller'], 'L2_ffn_f1': _L2_ffn_in['f1'], 'L2_ffn_f2': _L2_ffn_in['f2'], 'L2_ffn_bias': _L2_ffn_in['bias'], 'L3_attn_W': _L3_attn_in['W'], 'L3_attn_b': _L3_attn_in['b'], 'L3_ffn_weight_int8': _L3_ffn_in['weight_int8'], 'L3_ffn_weight_scale': _L3_ffn_in['weight_scale'], 'L3_ffn_bias': _L3_ffn_in['bias']}

def reference(x, L0_tok_W, L0_tok_b, L0_attn_qkv_w, L0_attn_q_norm_w, L0_attn_q_norm_b, L0_attn_k_norm_w, L0_attn_k_norm_b, L0_attn_proj_w, L0_attn_proj_b, L0_ffn_norm_scale, L0_ffn_w_router, L0_ffn_w_up, L0_ffn_w_down, L1_attn_Wq, L1_attn_Wk, L1_attn_Wv, L1_attn_Wo, L1_attn_Wbet, L1_attn_Wf, L1_attn_norm_w, L1_ffn_W_r, L1_ffn_W_k, L1_ffn_W_v, L1_ffn_mu_r, L1_ffn_mu_k, L2_attn_w_qkv, L2_attn_w_out, L2_ffn_controller, L2_ffn_f1, L2_ffn_f2, L2_ffn_bias, L3_attn_W, L3_attn_b, L3_ffn_weight_int8, L3_ffn_weight_scale, L3_ffn_bias):
    import jax
    import jax.numpy as jnp

    def _L0_tok_ref(x, W, b):
        import jax, jax.numpy as jnp
        import numpy as np
        P = 16
        B, C, H, Wd = x.shape
        h, w = (H // P, Wd // P)
        patches = x.reshape(B, C, h, P, w, P).transpose(0, 2, 4, 1, 3, 5)
        patches = patches.reshape(B, h * w, C * P * P)
        return jnp.einsum('bld,ed->ble', patches, W) + b

    def _L0_attn_ref(x, qkv_w, q_norm_w, q_norm_b, k_norm_w, k_norm_b, proj_w, proj_b):
        import jax, jax.numpy as jnp
        import numpy as np
        DIM = 256
        H = 16
        D = DIM // H
        SCALE = D ** (-0.5)
        EPS = 1e-05

        def _layernorm(x, w, b):
            xf = x.astype(jnp.float32)
            mu = xf.mean(-1, keepdims=True)
            var = xf.var(-1, keepdims=True)
            y = (xf - mu) / jnp.sqrt(var + EPS) * w.astype(jnp.float32) + b.astype(jnp.float32)
            return y.astype(x.dtype)
        B, N, C = x.shape
        qkv = x @ qkv_w.T
        qkv = qkv.reshape(B, N, 3, H, D).transpose(2, 0, 3, 1, 4)
        q, k, v = (qkv[0], qkv[1], qkv[2])
        q = _layernorm(q, q_norm_w, q_norm_b)
        k = _layernorm(k, k_norm_w, k_norm_b)
        k = k - k.mean(-2, keepdims=True)
        attn = jnp.einsum('bhnd,bhmd->bhnm', q * SCALE, k)
        attn = attn - attn.max(-1, keepdims=True)
        attn = jax.nn.softmax(attn, axis=-1)
        out = jnp.einsum('bhnm,bhmd->bhnd', attn, v)
        out = out.transpose(0, 2, 1, 3).reshape(B, N, C)
        return out @ proj_w.T + proj_b

    def _L0_ffn_ref(x, norm_scale, w_router, w_up, w_down):
        import jax, jax.numpy as jnp
        import numpy as np
        EPS = 1e-06
        TOP_K = 2

        def rms_norm(x, scale, eps=EPS):
            xf = x.astype(jnp.float32)
            mean_sq = jnp.mean(xf * xf, axis=-1, keepdims=True)
            return (xf * (scale.astype(jnp.float32) * jax.lax.rsqrt(mean_sq + eps))).astype(x.dtype)
        skip = x
        xn = rms_norm(x, norm_scale)
        scores = jnp.einsum('bsd,ed->bse', xn, w_router)
        _, ids = jax.lax.top_k(scores, TOP_K)
        probs = jax.nn.softmax(scores, axis=-1)
        c = jnp.take_along_axis(probs, ids, axis=-1)
        h = jnp.einsum('bsd,ehd->bseh', xn, w_up)
        val, gate = jnp.split(h, 2, axis=-1)
        h = val * jax.nn.silu(gate)
        y = jnp.einsum('bseh,edh->bsed', h, w_down)
        yk = jnp.take_along_axis(y, ids[..., None], axis=2)
        out = jnp.sum(yk * c[..., None], axis=2)
        return out + skip

    def _L1_attn_ref(x, Wq, Wk, Wv, Wo, Wbet, Wf, norm_w):
        import jax, jax.numpy as jnp
        import numpy as np
        EPS = 1e-06
        b, n, d = x.shape
        h = Wbet.shape[1]
        hd = d // h
        q = jax.nn.silu(x @ Wq).reshape(b, n, h, hd)
        k = jax.nn.silu(x @ Wk).reshape(b, n, h, hd)
        k = k * jax.lax.rsqrt(jnp.sum(k * k, -1, keepdims=True) + 1e-12)
        v = (x @ Wv).reshape(b, n, h, hd)
        beta = 2.0 * jax.nn.sigmoid(x @ Wbet)
        a = jax.nn.sigmoid(x @ Wf)

        def step(S, inp):
            qt, kt, vt, at, bt = inp
            Sd = at[..., None, None] * S
            u = vt - jnp.einsum('bhk,bhkv->bhv', kt, Sd)
            Sn = Sd + bt[..., None, None] * kt[..., None] * u[:, :, None, :]
            o = jnp.einsum('bhk,bhkv->bhv', qt, Sn)
            return (Sn, o)
        tfirst = lambda z: jnp.moveaxis(z, 1, 0)
        S0 = jnp.zeros((b, h, hd, hd), x.dtype)
        _, o = jax.lax.scan(step, S0, (tfirst(q), tfirst(k), tfirst(v), tfirst(a), tfirst(beta)))
        o = jnp.moveaxis(o, 0, 1)
        o = o * jax.lax.rsqrt(jnp.mean(o * o, -1, keepdims=True) + EPS)
        o = o.reshape(b, n, d) * norm_w
        return o @ Wo

    def _L1_ffn_ref(x, W_r, W_k, W_v, mu_r, mu_k):
        import jax, jax.numpy as jnp
        import numpy as np
        DIM = 256

        def _reference_tuple_inner(x, W_r, W_k, W_v, mu_r, mu_k):
            B, T, C = x.shape
            x_prev = jnp.concatenate([jnp.zeros((B, 1, C), x.dtype), x[:, :-1, :]], axis=1)
            xr = mu_r * x + (1.0 - mu_r) * x_prev
            xk = mu_k * x + (1.0 - mu_k) * x_prev
            r = jax.nn.sigmoid(jnp.einsum('btc,dc->btd', xr, W_r))
            k = jnp.einsum('btc,dc->btd', xk, W_k)
            k_act = jnp.square(jax.nn.relu(k))
            out = r * jnp.einsum('btc,dc->btd', k_act, W_v)
            new_state = x[:, -1, :]
            return (out, new_state)
        return _reference_tuple_inner(x, W_r, W_k, W_v, mu_r, mu_k)[0]

    def _L2_attn_ref(x, w_qkv, w_out):
        import jax, jax.numpy as jnp
        import numpy as np
        import math
        D_MODEL = 256
        NUM_HEADS = 16
        HEAD_DIM = D_MODEL // NUM_HEADS
        B, S, _ = x.shape
        qkv = jnp.einsum('bsi,oi->bso', x, w_qkv)
        q, k, v = jnp.split(qkv, 3, axis=-1)

        def to_heads(t):
            return t.reshape(B, S, NUM_HEADS, HEAD_DIM).transpose(0, 2, 1, 3)
        q, k, v = (to_heads(q), to_heads(k), to_heads(v))
        scale = 1.0 / math.sqrt(HEAD_DIM)
        logits = jnp.einsum('bhsd,bhtd->bhst', q, k) * scale
        mask = jnp.tril(jnp.ones((S, S), dtype=bool))
        neg_inf = jnp.finfo(jnp.float32).min
        logits = jnp.where(mask, logits, neg_inf)
        probs = jax.nn.softmax(logits, axis=-1)
        probs = probs * mask.astype(probs.dtype)
        out = jnp.einsum('bhst,bhtd->bhsd', probs, v)
        out = out.transpose(0, 2, 1, 3).reshape(B, S, D_MODEL)
        return jnp.einsum('bsi,oi->bso', out, w_out)

    def _L2_ffn_ref(x, controller, f1, f2, bias):
        import jax, jax.numpy as jnp
        import numpy as np
        DM, NE, ES, ESZ = (256, 16, 4, 64)
        BATCH, SEQ = (8, 512)
        ne = controller.shape[1]
        d = x.shape[-1]
        grouped = x.reshape(x.shape[:-2] + (-1, ne, d))
        logits = jnp.einsum('...btd,des->...btes', grouped, controller)
        tie = jnp.linspace(0.0, 1e-06, ne, dtype=logits.dtype).reshape(ne, 1, 1)
        logits = logits + tie
        perm = (logits == jnp.max(logits, axis=-3, keepdims=True)).astype(x.dtype)
        sel = jnp.einsum('...btd,...btes->...besd', grouped, perm)
        inner = jax.nn.relu(jnp.einsum('...besd,desf->...besf', sel, f1) + bias)
        inter = jnp.einsum('...besf,esfd->...besd', inner, f2)
        out = jnp.einsum('...besd,...btes->...btd', inter, perm)
        return out.reshape(x.shape)

    def _L3_attn_ref(x, W, b):
        import jax, jax.numpy as jnp
        import numpy as np
        B, K, D = (4, 2048, 256)
        lam = jax.nn.sigmoid(jnp.einsum('bkd,ed->bke', x, W) + b)
        u_gated = (1.0 - lam) * x

        def step(s, inputs):
            lam_t, ug_t = inputs
            s = lam_t * s + ug_t
            return (s, s)
        s0 = jnp.zeros((x.shape[0], x.shape[2]), dtype=x.dtype)
        _, ys = jax.lax.scan(step, s0, (jnp.swapaxes(lam, 0, 1), jnp.swapaxes(u_gated, 0, 1)))
        return jnp.swapaxes(ys, 0, 1)

    def _L3_ffn_ref(x, weight_int8, weight_scale, bias):
        import jax, jax.numpy as jnp
        import numpy as np
        EPS = 1e-05
        B, S, K = x.shape
        x2 = x.reshape(-1, K)
        x_scale = jnp.maximum(jnp.abs(x2).max() / 127.0, EPS)
        x_int8 = jnp.clip(jnp.round(x2 / x_scale), -128, 127).astype(jnp.int8)
        acc_i32 = jax.lax.dot_general(x_int8, weight_int8.T, dimension_numbers=(((1,), (0,)), ((), ())), preferred_element_type=jnp.int32)
        out = acc_i32.astype(jnp.float32) * x_scale * weight_scale.T
        out = out + bias
        return out.reshape(B, S, -1)
    h = _L0_tok_ref(x, L0_tok_W, L0_tok_b)
    h = _layernorm(h + _L0_attn_ref(h, L0_attn_qkv_w, L0_attn_q_norm_w, L0_attn_q_norm_b, L0_attn_k_norm_w, L0_attn_k_norm_b, L0_attn_proj_w, L0_attn_proj_b), axis=-1)
    h = _layernorm(h + _L0_ffn_ref(h, L0_ffn_norm_scale, L0_ffn_w_router, L0_ffn_w_up, L0_ffn_w_down), axis=-1)
    h = _layernorm(h + _L1_attn_ref(h, L1_attn_Wq, L1_attn_Wk, L1_attn_Wv, L1_attn_Wo, L1_attn_Wbet, L1_attn_Wf, L1_attn_norm_w), axis=-1)
    h = _layernorm(h + _L1_ffn_ref(h, L1_ffn_W_r, L1_ffn_W_k, L1_ffn_W_v, L1_ffn_mu_r, L1_ffn_mu_k), axis=-1)
    h = _layernorm(h + _L2_attn_ref(h, L2_attn_w_qkv, L2_attn_w_out), axis=-1)
    h = _layernorm(h + _L2_ffn_ref(h, L2_ffn_controller, L2_ffn_f1, L2_ffn_f2, L2_ffn_bias), axis=-1)
    h = _layernorm(h + _L3_attn_ref(h, L3_attn_W, L3_attn_b), axis=-1)
    h = _layernorm(h + _L3_ffn_ref(h, L3_ffn_weight_int8, L3_ffn_weight_scale, L3_ffn_bias), axis=-1)
    return h

_drawn_inputs = setup_inputs


def setup_inputs(seed=0):
    import zlib

    import numpy as np

    out = dict(_drawn_inputs(seed))
    spreads = {'L0_attn_q_norm_w': (1.0, 0.2),
     'L0_attn_q_norm_b': (0.0, 0.276),
     'L0_attn_k_norm_w': (1.0, 0.2),
     'L0_attn_k_norm_b': (0.0, 0.8),
     'L0_attn_proj_b': (0.0, 0.1),
     'L0_ffn_norm_scale': (1.0, 0.6),
     'L1_attn_norm_w': (1.0, 0.2)}
    factors = {'L0_ffn_w_router': 7.589,
     'L0_ffn_w_up': 6.961,
     'L0_ffn_w_down': 7.109,
     'L1_ffn_mu_r': 4.962,
     'L2_ffn_bias': 8.0,
     'L3_attn_b': 8.0,
     'L3_ffn_bias': 5.836}
    for name, (base, spread) in spreads.items():
        noise = np.random.default_rng([zlib.crc32(name.encode()), seed]).standard_normal(out[name].shape)
        drawn = base * np.exp(spread * noise) if base else spread * noise
        out[name] = jnp.asarray(drawn.astype(out[name].dtype))
    for name, factor in factors.items():
        out[name] = (out[name] * factor).astype(out[name].dtype)
    return out
```

```python
from contextlib import ExitStack

import concourse.bass as bass
from concourse import mybir

ALU = mybir.AluOpType
ACT = mybir.ActivationFunctionType
AX = mybir.AxisListType
F32 = mybir.dt.float32
BF16 = mybir.dt.bfloat16
I32 = mybir.dt.int32
U32 = mybir.dt.uint32
I8 = mybir.dt.int8

P = 128
D = 256
DC = D // P
IMAGES = 32
TOK = 64
T = IMAGES * TOK // P
PAIR = 2
TURNS = T // PAIR
HEADS = 16
HD = D // HEADS
SLOT = 32
HC = HEADS * SLOT // P
HR = P // SLOT
PATCH = 768
PC = PATCH // P
E = 8
HID = 704
HIDC = -(-HID // P)
HLAST = HID - (HIDC - 1) * P
SLOTS = 40

ME = 64
FE = 64
GROUP = 16
GPT = P // GROUP
CG = 4
MAGIC = 12582912.0


class Tally:

    def __init__(self, eng, sem, turn=0, per=0):
        self.eng, self.sem, self.base, self.n = eng, sem, turn * per, 0

    def mark(self, ins):
        ins.then_inc(self.sem, 1)
        self.n += 1

    def settle(self):
        self.eng.wait_ge(self.sem, self.base + self.n)


def starts_free(eng, sem, n):
    eng.sem_inc(sem, n)


def bcast(ap, axis, n):
    ap = ap.unsqueeze(axis)
    shape = [int(s) for s in ap.shape]
    shape[axis] = n
    return ap.to_broadcast(shape)


class Sems:

    def __init__(self, nc, ctx, phase):
        self.nc, self.phase, self.made = nc, phase, {}
        ctx.callback(self.retire)

    def retire(self):
        self.nc.clear_and_free_semaphores(list(self.made.values()))
        self.nc.all_engine_barrier()

    def __call__(self, name):
        if name not in self.made:
            self.made[name] = self.nc.alloc_semaphore(f"{self.phase}_{name}")
        return self.made[name]


def kept(dve, dst, src):
    return dve.tensor_scalar(dst, src, 1.0, None, ALU.mult)


def transposes(pe, out, src, ident, chunks):
    for c in range(chunks):
        ins = pe.transpose(out[:, c, :], src[:, c * P:(c + 1) * P], ident)
    return ins



def attention_pe(pe, sem, turn, p, s, B, ident, ident_bf, mask, maskT, stage):
    v = turn * PAIR + p + 1
    if stage == "scores":
        pe.wait_ge(sem("k_slots"), v)
        transposes(pe, B[3].rearrange("p (c n) -> p c n", c=HC), s["k_ext"], ident, HC).then_inc(sem("kT_made"), 1)
        pe.wait_ge(sem("q_slots"), v)
        transposes(pe, B[2].rearrange("p (c n) -> p c n", c=HC), s["q_ext"], ident, HC).then_inc(sem("qT_made"), 1)
    if stage in ("scores_a", "scores_b", "shifted_a", "shifted_b"):
        half = stage[-1] == "b"
        if stage == "scores_a":
            pe.wait_ge(sem("kT_copied"), v)
            pe.wait_ge(sem("qT_copied"), v)
        if stage == "shifted_a":
            pe.wait_ge(sem("qmT_copied"), v)
        first = stage.startswith("scores")
        rows = HD if first else HD + 1
        for k in range(2):
            r = 2 * half + k
            bank = B[2 * half + k].rearrange("p (c n) -> p c n", c=HC)
            pe.matmul(B[2 * half + k], ident_bf, mask if first else maskT, start=True, stop=False)
            for c in range(HC):
                a = s["qT"][SLOT * r:SLOT * r + rows, c, :]
                b = s["kT"][SLOT * r:SLOT * r + rows, c, :]
                ins = pe.matmul(bank[:, c, :], a if first else b, b if first else a,
                                start=False, stop=(c == HC - 1))
        ins.then_inc(sem("scores_made" if first else "shifted_made"), 1)
    if stage == "again":
        pe.wait_ge(sem("max_in_q"), v)
        transposes(pe, B[0].rearrange("p (c n) -> p c n", c=HC), s["q_ext"], ident, HC).then_inc(sem("qmT_made"), 1)
    if stage == "pv":
        pe.wait_ge(sem("probs"), turn * 4 + 2 + p + 1)
        pe.wait_ge(sem("v_slots"), v)
        oT = B[0].rearrange("p (c n) -> p c n", c=HC)
        for h in range(HEADS):
            c, r = h // HR, h % HR
            ins = pe.matmul(oT[SLOT * r:SLOT * (r + 1), c, :], s["v_ext"][:, h * SLOT:(h + 1) * SLOT],
                            s["PT"][:, h, :], start=True, stop=True, skip_group_check=True)
        ins.then_inc(sem("oT_made"), 1)
    if stage == "turn_back":
        pe.wait_ge(sem("oT_copied"), v)
        transposes(pe, B[1].rearrange("p (c n) -> p c n", c=HC), s["oT"], ident, HC).then_inc(sem("o_made"), 1)
    if stage == "o_features":
        pe.wait_ge(sem("o_divided"), v)
        transposes(pe, B[2][:, 0:D].rearrange("p (c n) -> p c n", c=DC), s["o"], ident, DC).then_inc(sem("of_made"), 1)


def heads(ap):
    return ap.rearrange("p (h x) -> p h x", x=SLOT)


def attention_act(act, sem, turn, p, s, B, stage, scale):
    v = turn * PAIR + p + 1
    if stage == "copies":
        act.wait_ge(sem("kT_made"), v)
        act.copy(s["kT"].rearrange("p c n -> p (c n)"), B[3]).then_inc(sem("kT_copied"), 1)
        act.wait_ge(sem("qT_made"), v)
        act.copy(s["qT"].rearrange("p c n -> p (c n)"), B[2]).then_inc(sem("qT_copied"), 1)
    if stage == "again":
        act.wait_ge(sem("qmT_made"), v)
        act.copy(s["qT"].rearrange("p c n -> p (c n)"), B[0]).then_inc(sem("qmT_copied"), 1)
    if stage in ("exp_a", "exp_b"):
        half = stage == "exp_b"
        act.wait_ge(sem("shifted_made"), turn * 4 + 2 * half + p + 1)
        pt = s["PT"].rearrange("p (c r) n -> p r c n", r=HR)
        for k in range(2):
            r = 2 * half + k
            ins = act.activation(pt[:, r, :, :], B[r].rearrange("p (c n) -> p c n", c=HC), ACT.Exp, scale=scale)
        ins.then_inc(sem("probs"), 1)
    if stage == "oT":
        act.wait_ge(sem("oT_made"), v)
        act.copy(s["oT"], B[0]).then_inc(sem("oT_copied"), 1)
    if stage == "of":
        act.wait_ge(sem("of_made"), v)
        act.copy(s["of"].rearrange("p c n -> p (c n)"), B[2][:, 0:D]).then_inc(sem("of_copied"), 1)


def attention_dve(dve, sem, turn, p, s, B, tally, stage):
    v = turn * PAIR + p + 1
    if stage == "max":
        neg = heads(s["q_ext"])[:, :, HD].rearrange("p (c r) -> p r c", r=HR)
        for half in range(2):
            dve.wait_ge(sem("scores_made"), turn * 4 + 2 * half + p + 1)
            for k in range(2):
                r = 2 * half + k
                ins = dve.tensor_reduce(neg[:, r, :], B[r].rearrange("p (c n) -> p c n", c=HC), AX.X, ALU.max,
                                        negate=True)
        ins.then_inc(sem("max_in_q"), 1)
    if stage == "divide":
        dve.wait_ge(sem("o_made"), v)
        o = heads(B[1])
        tally.mark(dve.reciprocal(s["den"], o[:, :, HD]))
        tally.settle()
        dve.tensor_tensor(s["o"].rearrange("p (h x) -> p h x", h=HEADS), o[:, :, 0:HD], bcast(s["den"], 2, HD),
                          ALU.mult).then_inc(sem("o_divided"), 1)


def vit_tower(nc, io, out):
    ctx = ExitStack()
    with ctx:
        def sb(name, shape, dt=F32, where=ctx):
            return where.enter_context(nc.sbuf_tensor(name, shape, dt))

        def dram(name, shape, dt=F32):
            return nc.dram_tensor(name, shape, dt).ap()

        banks = ctx.enter_context(nc.psum_tensor("banks", [P, 8, 512], F32))
        B = [[banks[:, 4 * p + k, :] for k in range(4)] for p in range(PAIR)]

        H = sb("H", [P, T, D])
        ident = sb("ident", [P, P])
        ident_bf = sb("ident_bf", [P, P], BF16)
        minus_half = sb("minus_half", [P, 2 * HEADS])
        loaded = ctx.enter_context(nc.semaphore("constants_loaded"))

        xn_rows = dram("xn_rows", (T * P, D))
        slot_rows = dram("slot_rows", (SLOTS * P, D))
        expert_rows = dram("expert_rows", (SLOTS * P, D))
        io["out"] = out

        with nc.Block() as block:
            @block.sync
            def _(sp):
                sp.dma_start(ident[:, :], io["ident"]).then_inc(loaded, 16)
                sp.dma_start(ident_bf[:, :], io["ident_bf"]).then_inc(loaded, 16)
                sp.wait_ge(loaded, 32)

            @block.vector
            def _(dve):
                dve.memset(minus_half[:, :], -0.5)

        scores_all = sb("scores_all", [P, T, E])
        embed_and_first_attention(nc, io, B, H, ident, ident_bf, minus_half, scores_all, xn_rows, slot_rows)
        first_experts(nc, io, banks, H, ident, minus_half, scores_all, xn_rows, slot_rows, expert_rows)
        vit_rest(nc, io, B, banks, H, ident, ident_bf, minus_half)


def rsqrt_pool(pool, sem_in, value, ap, half, sem_out):
    pool.wait_ge(sem_in, value)
    pool.tensor_tensor(ap, ap, half, ALU.pow).then_inc(sem_out, 1)


def attention_buffers(nc, ctx, tag):
    def sb(name, shape):
        return ctx.enter_context(nc.sbuf_tensor(f"{name}_{tag}", shape, F32))
    s = {}
    s["q_ext"] = sb("q_ext", [P, HEADS * SLOT])[:, :]
    s["k_ext"] = sb("k_ext", [P, HEADS * SLOT])[:, :]
    s["v_ext"] = sb("v_ext", [P, HEADS * SLOT])[:, :]
    s["qT"] = sb("qT", [P, HC, P])[:, :, :]
    s["kT"] = sb("kT", [P, HC, P])[:, :, :]
    s["PT"] = sb("PT", [P, HEADS, P])[:, :, :]
    s["oT"] = sb("oT", [P, HEADS * SLOT])[:, :]
    s["den"] = sb("den", [P, HEADS])[:, :]
    s["o"] = sb("o", [P, D])[:, :]
    s["of"] = sb("of", [P, DC, P])[:, :, :]
    s["xT"] = sb("xT", [P, DC, P])[:, :, :]
    s["x"] = sb("x", [P, D])[:, :]
    s["r"] = sb("r", [P, D])[:, :]
    s["stats"] = sb("stats", [P, 6])[:, :]
    s["agg"] = sb("agg", [P, 2])[:, :]
    s["pace"] = sb("pace", [P, 1])[:, :]
    return s


def clear_slots(dve, s, tally):
    for p in range(PAIR):
        for name in ("q_ext", "k_ext", "v_ext"):
            tally.mark(dve.memset(s[p][name], 0.0))
    tally.settle()
    for p in range(PAIR):
        for name in ("k_ext", "v_ext"):
            tally.mark(dve.memset(heads(s[p][name])[:, :, HD], 1.0))
    tally.settle()


def embed_and_first_attention(nc, io, B, H, ident, ident_bf, minus_half, scores_all, xn_rows, slot_rows):
    with ExitStack() as ctx:
        def sb(name, shape, dt=F32):
            return ctx.enter_context(nc.sbuf_tensor(name, shape, dt))

        sem = Sems(nc, ctx, "a")
        w_tok = sb("w_tok", [P, PC, D])
        b_tok = sb("b_tok", [P, D])
        w_qkv = sb("w_qkv", [P, DC, 3 * D])
        qk_w = sb("qk_w", [P, 2 * D])
        qk_b = sb("qk_b", [P, 2 * D])
        w_proj = sb("w_proj", [P, DC, D])
        b_proj = sb("b_proj", [P, D])
        token_mean = sb("token_mean", [P, P])
        rms_w = sb("rms_w", [P, D])
        w_router = sb("w_router", [P, DC, E])
        mask = sb("mask", [P, HC * P], BF16)
        zeros = sb("zeros", [P, 4 * D])
        s = [attention_buffers(nc, ctx, f"a{p}") for p in range(PAIR)]
        patches = [sb(f"patches{p}", [P, PC, P]) for p in range(PAIR)]
        cen = [sb(f"cen{p}", [P, 2 * D]) for p in range(PAIR)]
        sq = [sb(f"sq{p}", [P, 2 * D]) for p in range(PAIR)]
        hs = sb("hs", [P, PAIR, 2, 2 * HEADS])
        rstd = sb("rstd", [P, PAIR, 2 * HEADS])
        newton = sb("newton", [P, PAIR, 2 * HEADS])
        kn = [sb(f"kn{p}", [P, D]) for p in range(PAIR)]
        xn = [sb(f"xn{p}", [P, D]) for p in range(PAIR)]
        xnT = [sb(f"xnT{p}", [P, DC, P]) for p in range(PAIR)]
        ss = [sb(f"ss{p}", [P, 1]) for p in range(PAIR)]
        weights = [(w_tok, "tok_w"), (b_tok, "tok_b"), (w_qkv, "qkv_w"), (qk_w, "qk_w"), (qk_b, "qk_b"),
                   (w_proj, "proj_w"), (b_proj, "proj_b"), (token_mean, "token_mean"), (rms_w, "rms_w"),
                   (w_router, "router_w"), (mask, "mask_pair")]
        tiles = range(PAIR)

        with nc.Block() as block:
            @block.sync
            def _(sp):
                for dst, name in weights:
                    sp.dma_start(dst[:], io[name]).then_inc(sem("weights"), 16)
                with sp.Fori(0, TURNS) as turn:
                    for p in tiles:
                        sp.wait_ge(sem("embedded"), turn * 2 + 2)
                        sp.dma_start(patches[p][:, :, :], io["patches"][bass.ds(turn * 2 + p, 1)]
                                     .rearrange("t p c n -> p (t c) n")).then_inc(sem(f"patches{p}"), 16)

            @block.gpsimd
            def _(pool):
                pool.memset(zeros[:, :], 0.0).then_inc(sem("zeroed"), 1)
                pool.wait_ge(sem("zeroed"), 1)
                for k in range(SLOTS // 4):
                    pool.dma_start(slot_rows[k * 4 * P:(k + 1) * 4 * P, :].rearrange("(p r) d -> p (r d)", r=4),
                                   zeros[:, :]).then_inc(sem("slots_cleared"), 16)
                with pool.Fori(0, TURNS) as turn:
                    for p in tiles:
                        t = turn * 2 + p
                        rsqrt_pool(pool, sem("ln_var"), t + 1, s[p]["agg"][:, 1:2], minus_half[:, 0:1], sem("ln_rstd"))
                    for p in tiles:
                        t = turn * 2 + p
                        rsqrt_pool(pool, sem("rms_ready"), t + 1, ss[p][:, :], minus_half[:, 0:1], sem("rms_rstd"))
                pool.wait_ge(sem("slots_cleared"), 16 * (SLOTS // 4))

            @block.tensor
            def _(pe):
                starts_free(pe, sem("embedded"), 2)
                pe.wait_ge(sem("weights"), 16 * len(weights))
                with pe.Fori(0, TURNS) as turn:
                    for p in tiles:
                        pe.wait_ge(sem(f"patches{p}"), turn * 16 + 16)
                        for c in range(PC):
                            ins = pe.matmul(B[p][2][:, 0:D], patches[p][:, c, :], w_tok[:, c, :],
                                            start=(c == 0), stop=(c == PC - 1))
                        ins.then_inc(sem("embedded"), 1)
                    for p in tiles:
                        t = turn * 2 + p
                        pe.wait_ge(sem("h_made"), t + 1)
                        transposes(pe, B[p][3][:, 0:D].rearrange("p (c n) -> p c n", c=DC), s[p]["x"], ident[:, :],
                                   DC).then_inc(sem("hT_made"), 1)
                    for p in tiles:
                        t = turn * 2 + p
                        pe.wait_ge(sem("hT_copied"), t + 1)
                        for c in range(DC):
                            pe.matmul(B[p][0], s[p]["xT"][:, c, :], w_qkv[:, c, 0:2 * D], start=(c == 0), stop=(c == 1))
                        for c in range(DC):
                            ins = pe.matmul(B[p][1][:, 0:D], s[p]["xT"][:, c, :], w_qkv[:, c, 2 * D:3 * D],
                                            start=(c == 0), stop=(c == 1))
                        ins.then_inc(sem("qkv_made"), 1)
                    for p in tiles:
                        t = turn * 2 + p
                        pe.wait_ge(sem("k_normed"), t + 1)
                        pe.matmul(B[p][3][:, 0:D], token_mean[:, :], kn[p][:, :], start=True,
                                  stop=True).then_inc(sem("k_mean_made"), 1)
                    for stage in ("scores", "scores_a", "scores_b", "again", "shifted_a", "shifted_b", "pv",
                                  "turn_back", "o_features"):
                        for p in tiles:
                            attention_pe(pe, sem, turn, p, s[p], B[p], ident[:, :], ident_bf[:, :], mask[:, :],
                                         mask[:, :], stage)
                    for p in tiles:
                        t = turn * 2 + p
                        pe.wait_ge(sem("of_copied"), t + 1)
                        for c in range(DC):
                            ins = pe.matmul(B[p][3][:, 0:D], s[p]["of"][:, c, :], w_proj[:, c, :], start=(c == 0),
                                            stop=(c == 1))
                        ins.then_inc(sem("projected"), 1)
                    for p in tiles:
                        t = turn * 2 + p
                        pe.wait_ge(sem("xn_made"), t + 1)
                        transposes(pe, B[p][0][:, 0:D].rearrange("p (c n) -> p c n", c=DC), xn[p], ident[:, :],
                                   DC).then_inc(sem("xnT_made"), 1)
                    for p in tiles:
                        t = turn * 2 + p
                        pe.wait_ge(sem("xnT_copied"), t + 1)
                        for c in range(DC):
                            ins = pe.matmul(B[p][1][:, 0:E], xnT[p][:, c, :], w_router[:, c, :], start=(c == 0),
                                            stop=(c == 1))
                        ins.then_inc(sem("routed"), 1)

            @block.scalar
            def _(act):
                for p in tiles:
                    starts_free(act, sem(f"xn_stored{p}"), 16)
                with act.Fori(0, TURNS) as turn:
                    for p in tiles:
                        t = turn * 2 + p
                        act.wait_ge(sem("hT_made"), t + 1)
                        act.copy(s[p]["xT"].rearrange("p c n -> p (c n)"), B[p][3][:, 0:D]).then_inc(sem("hT_copied"), 1)
                    for p in tiles:
                        t = turn * 2 + p
                        act.wait_ge(sem("qkv_made"), t + 1)
                        act.wait_ge(sem("h_made"), t + 1)
                        act.copy(heads(s[p]["v_ext"])[:, :, 0:HD], B[p][1][:, 0:D].rearrange("p (h x) -> p h x", x=HD)
                                 ).then_inc(sem("v_slots"), 1)
                    for p in tiles:
                        t = turn * 2 + p
                        act.wait_ge(sem("centred"), t + 1)
                        act.square(sq[p][:, :], cen[p][:, :]).then_inc(sem("squared"), 1)
                    rsqrt_refined(act, None, sem, None, hs[:, :, 1, :], rstd[:, :, :], None, "head_var", turn + 1)
                    for stage in ("copies", "again", "exp_a", "exp_b", "oT", "of"):
                        for p in tiles:
                            attention_act(act, sem, turn, p, s[p], B[p], stage, HD ** -0.5)
                    for p in tiles:
                        t = turn * 2 + p
                        act.wait_ge(sem("ln_done"), t + 1)
                        act.activation(sq[p][:, 0:D], s[p]["x"], ACT.Square, accum_out=ss[p][:, :]
                                       ).then_inc(sem("rms_sum"), 1)
                    for p in tiles:
                        t = turn * 2 + p
                        act.wait_ge(sem("xnT_made"), t + 1)
                        act.copy(xnT[p][:, :, :].rearrange("p c n -> p (c n)"), B[p][0][:, 0:D]
                                 ).then_inc(sem("xnT_copied"), 1)
                        act.dma_start(xn_rows[bass.ds(t * P, P), :], xn[p][:, :]).then_inc(sem(f"xn_stored{p}"), 16)
                for p in tiles:
                    act.wait_ge(sem(f"xn_stored{p}"), 16 * TURNS + 16)

            @block.vector
            def _(dve):
                once = Tally(dve, sem("cleared"))
                clear_slots(dve, s, once)
                dve.wait_ge(sem("weights"), 16 * len(weights))
                with dve.Fori(0, TURNS) as turn:
                    tally = Tally(dve, sem("dve"), turn, 29)
                    for p in tiles:
                        t = turn * 2 + p
                        dve.wait_ge(sem("embedded"), t + 3)
                        dve.tensor_tensor(s[p]["x"], B[p][2][:, 0:D], b_tok[:, :], ALU.add).then_inc(sem("h_made"), 1)
                    h16 = [dict(x=lambda ap: ap.rearrange("p (h x) -> p h x", x=HD))] * 2
                    v3 = h16[0]["x"]
                    for p in tiles:
                        t = turn * 2 + p
                        dve.wait_ge(sem("qkv_made"), t + 1)
                        tally.mark(dve.tensor_reduce(hs[:, p, 0, :], v3(B[p][0]), AX.X, ALU.add))
                    tally.settle()
                    for p in tiles:
                        tally.mark(dve.tensor_scalar(hs[:, p, 0, :], hs[:, p, 0, :], 1.0 / HD, None, ALU.mult))
                    tally.settle()
                    for p in tiles:
                        dve.tensor_tensor(v3(cen[p][:, :]), v3(B[p][0]), bcast(hs[:, p, 0, :], 2, HD),
                                          ALU.subtract).then_inc(sem("centred"), 1)
                    for p in tiles:
                        t = turn * 2 + p
                        dve.wait_ge(sem("squared"), t + 1)
                        tally.mark(dve.tensor_reduce(hs[:, p, 1, :], v3(sq[p][:, :]), AX.X, ALU.add))
                    tally.settle()
                    dve.tensor_scalar(hs[:, :, 1, :], hs[:, :, 1, :], 1.0 / HD, 1e-5, ALU.mult,
                                      ALU.add).then_inc(sem("head_var_x"), 1)
                    rsqrt_refined(None, dve, sem, tally, hs[:, :, 1, :], rstd[:, :, :], newton[:, :, :], "head_var",
                                  turn + 1)
                    for p in tiles:
                        tally.mark(dve.tensor_tensor(v3(cen[p][:, :]), v3(cen[p][:, :]), bcast(rstd[:, p, :], 2, HD),
                                                     ALU.mult))
                    tally.settle()
                    for p in tiles:
                        tally.mark(dve.tensor_tensor(cen[p][:, :], cen[p][:, :], qk_w[:, :], ALU.mult))
                    tally.settle()
                    for p in tiles:
                        dve.tensor_tensor(kn[p][:, :], cen[p][:, D:2 * D], qk_b[:, D:2 * D], ALU.add
                                          ).then_inc(sem("k_normed"), 1)
                        dve.tensor_tensor(heads(s[p]["q_ext"])[:, :, 0:HD], v3(cen[p][:, 0:D]), v3(qk_b[:, 0:D]),
                                          ALU.add).then_inc(sem("q_slots"), 1)
                    for p in tiles:
                        t = turn * 2 + p
                        dve.wait_ge(sem("k_mean_made"), t + 1)
                        dve.wait_ge(sem("k_normed"), t + 1)
                        dve.tensor_tensor(heads(s[p]["k_ext"])[:, :, 0:HD], v3(kn[p][:, :]), v3(B[p][3][:, 0:D]),
                                          ALU.subtract).then_inc(sem("k_slots"), 1)
                    for stage in ("max", "divide"):
                        for p in tiles:
                            attention_dve(dve, sem, turn, p, s[p], B[p], tally, stage)
                    for p in tiles:
                        t = turn * 2 + p
                        dve.wait_ge(sem("projected"), t + 1)
                        tally.mark(dve.tensor_tensor(s[p]["r"], B[p][3][:, 0:D], b_proj[:, :], ALU.add))
                    tally.settle()
                    for p in tiles:
                        tally.mark(dve.tensor_tensor(s[p]["r"], s[p]["r"], s[p]["x"], ALU.add))
                    tally.settle()
                    layer_norm(dve, sem, turn, tally, s, 1e-5, [s[p]["x"] for p in tiles])
                    for p in tiles:
                        t = turn * 2 + p
                        dve.wait_ge(sem("ln_done"), t + 1)
                        tally.mark(kept(dve, H[:, bass.ds(t, 1), :].rearrange("p t d -> p (t d)"), s[p]["x"]))
                    for p in tiles:
                        t = turn * 2 + p
                        dve.wait_ge(sem("rms_sum"), t + 1)
                        dve.tensor_scalar(ss[p][:, :], ss[p][:, :], 1.0 / D, 1e-6, ALU.mult,
                                          ALU.add).then_inc(sem("rms_ready"), 1)
                    for p in tiles:
                        t = turn * 2 + p
                        dve.wait_ge(sem("rms_rstd"), t + 1)
                        dve.wait_ge(sem(f"xn_stored{p}"), turn * 16 + 16)
                        dve.scalar_tensor_tensor(out=xn[p][:, :], in0=s[p]["x"], scalar=ss[p][:, :], in1=rms_w[:, :],
                                                 op0=ALU.mult, op1=ALU.mult).then_inc(sem("xn_made"), 1)
                    for p in tiles:
                        t = turn * 2 + p
                        dve.wait_ge(sem("routed"), t + 1)
                        tally.mark(kept(dve, scores_all[:, bass.ds(t, 1), :].rearrange("p t d -> p (t d)"),
                                                   B[p][1][:, 0:E]))
                    tally.settle()
                    assert tally.n == 29, tally.n


def layer_norm(dve, sem, turn, tally, s, eps, dst, name="ln"):
    for p in range(PAIR):
        tally.mark(dve.bn_stats(s[p]["stats"], s[p]["r"]))
    tally.settle()
    dve.memset(s[0]["pace"], 0.0)
    for p in range(PAIR):
        tally.mark(dve.bn_aggr(s[p]["agg"], s[p]["stats"]))
    tally.settle()
    for p in range(PAIR):
        dve.tensor_scalar(s[p]["agg"][:, 1:2], s[p]["agg"][:, 1:2], eps, None, ALU.add).then_inc(sem(name + "_var"), 1)
    for p in range(PAIR):
        dve.wait_ge(sem(name + "_rstd"), turn * 2 + p + 1)
        dve.tensor_scalar(dst[p], s[p]["r"], s[p]["agg"][:, 0:1], s[p]["agg"][:, 1:2], ALU.subtract,
                          ALU.mult).then_inc(sem(name + "_done"), 1)


def first_experts(nc, io, banks, H, ident, minus_half, scores_all, xn_rows, slot_rows, expert_rows):
    with ExitStack() as ctx:
        def sb(name, shape, dt=F32, where=ctx):
            return where.enter_context(nc.sbuf_tensor(name, shape, dt))

        sem = Sems(nc, ctx, "m")
        w_up = sb("w_up", [P, E * DC, 2 * HID])
        w_down = sb("w_down", [P, E * HIDC, D])
        slot = sb("slot", [P, 2, T], I32)
        gate = sb("gate", [P, 2, T])
        tile_at = sb("tile_at", [P, SLOTS], I32)
        route(nc, io, sem, banks, scores_all, slot, gate, tile_at, w_up, w_down)
        deal_rows(nc, sem, xn_rows, slot_rows, slot)
        run_experts(nc, io, sem, banks, ident, w_up, w_down, tile_at, slot_rows, expert_rows)
        collect_rows(nc, sem, H, minus_half, gate, slot, expert_rows)


def route(nc, io, sem, banks, scores_all, slot, gate, tile_at, w_up, w_down):
    with ExitStack() as ctx:
        def sb(name, shape, dt=F32):
            return ctx.enter_context(nc.sbuf_tensor(name, shape, dt))

        top = sb("top", [P, T, 8])
        which = sb("which", [P, T, 8], U32)
        which_f = sb("which_f", [P, T, 2])
        ramp = sb("ramp", [P, E])
        before = sb("before", [P, P])
        ones = sb("ones", [P, P])
        keep = sb("keep", [P, E * T])
        keep_e = sb("keep_e", [P, E])
        full = sb("full", [P, T])
        tile_no = sb("tile_no", [P, SLOTS])
        hot = sb("hot", [P, 2, T, E])
        both = sb("both", [P, T, E])
        shifted = sb("shifted", [P, T, E])
        total = sb("total", [P, T])
        tiles_before = sb("tiles_before", [P, E, T])
        per_tile = sb("per_tile", [P, E, T])
        cmp = sb("cmp", [P, E, T])
        need = sb("need", [P, E])
        ends = sb("ends", [P, E])
        first = sb("first", [P, E])
        where = sb("where", [P, T, E])
        picked = sb("picked", [P, 2, T, E])
        slot_f = sb("slot_f", [P, 2, T])
        past = sb("past", [P, SLOTS, E])
        tile_f = sb("tile_f", [P, SLOTS])
        constants = [(ramp, "ramp"), (before, "before"), (ones, "ones"), (keep, "keep"), (keep_e, "keep_e"),
                     (full, "full"), (tile_no, "tile_no")]
        rank_bank, total_bank = banks[:, 0, 0:T * E], banks[:, 1, 0:T * E]

        with nc.Block() as block:
            @block.sync
            def _(sp):
                for dst, name in constants:
                    sp.dma_start(dst[:], io[name]).then_inc(sem("constants"), 16)
                for e in range(E):
                    sp.dma_start(w_up[:, DC * e:DC * (e + 1), :], io["up_w"][:, e, :, :]).then_inc(sem("up"), 16)

            @block.scalar
            def _(act):
                for e in range(E):
                    act.dma_start(w_down[:, HIDC * e:HIDC * e + HIDC - 1, :], io["down_w"][:, e, 0:HIDC - 1, :]
                                  ).then_inc(sem("down"), 16)
                    act.dma_start(w_down[0:HLAST, HIDC * (e + 1) - 1, :], io["down_w"][0:HLAST, e, HIDC - 1, :]
                                  ).then_inc(sem("down"), 16)
                act.wait_ge(sem("scores_shifted"), 1)
                act.activation(shifted[:, :, :], shifted[:, :, :], ACT.Exp).then_inc(sem("scores_exp"), 1)
                act.wait_ge(sem("tops_shifted"), 1)
                act.activation(gate[:, 1, :], gate[:, 1, :], ACT.Exp).then_inc(sem("tops_exp"), 1)

            @block.tensor
            def _(pe):
                pe.wait_ge(sem("constants"), 16 * len(constants))
                pe.wait_ge(sem("both_hot"), 1)
                m = both[:, :, :].rearrange("p t e -> p (t e)")
                pe.matmul(rank_bank, before[:, :], m, start=True, stop=True)
                pe.matmul(total_bank, ones[:, :], m, start=True, stop=True).then_inc(sem("ranks"), 1)

            @block.vector
            def _(dve):
                tally = Tally(dve, sem("dve_route"))
                for t in range(T):
                    tally.mark(dve.max(top[:, t, :], scores_all[:, t, :]))
                tally.settle()
                for t in range(T):
                    tally.mark(dve.max_index(which[:, t, :], top[:, t, :], scores_all[:, t, :]))
                dve.tensor_tensor(shifted[:, :, :], scores_all[:, :, :], bcast(top[:, :, 0], 2, E), ALU.subtract
                                  ).then_inc(sem("scores_shifted"), 1)
                dve.tensor_tensor(gate[:, 1, :], top[:, :, 1], top[:, :, 0], ALU.subtract
                                  ).then_inc(sem("tops_shifted"), 1)
                tally.settle()
                tally.mark(dve.tensor_copy(which_f[:, :, :], which[:, :, 0:2]))
                tally.settle()
                dve.wait_ge(sem("constants"), 16 * len(constants))
                for k in range(2):
                    tally.mark(dve.tensor_tensor(hot[:, k, :, :], bcast(ramp[:, :], 1, T), bcast(which_f[:, :, k], 2, E),
                                                 ALU.is_equal))
                tally.settle()
                dve.tensor_tensor(both[:, :, :], hot[:, 0, :, :], hot[:, 1, :, :], ALU.add).then_inc(sem("both_hot"), 1)
                dve.wait_ge(sem("scores_exp"), 1)
                dve.wait_ge(sem("tops_exp"), 1)
                tally.mark(dve.tensor_reduce(total[:, :], shifted[:, :, :], AX.X, ALU.add))
                tally.settle()
                tally.mark(dve.reciprocal(gate[:, 0, :], total[:, :]))
                tally.settle()
                tally.mark(dve.tensor_tensor(gate[:, 1, :], gate[:, 1, :], gate[:, 0, :], ALU.mult))
                dve.wait_ge(sem("ranks"), 1)
                tally.mark(dve.tensor_copy(per_tile[:, :, :], total_bank.rearrange("p (t e) -> p e t", e=E)))
                tally.settle()
                tally.mark(dve.tensor_tensor_scan(tiles_before[:, :, :].rearrange("p e t -> p (e t)"), keep[:, :],
                                                  per_tile[:, :, :].rearrange("p e t -> p (e t)"), 0.0,
                                                  ALU.mult, ALU.add))
                tally.settle()
                tally.mark(dve.tensor_tensor(cmp[:, :, :], bcast(tiles_before[:, :, T - 1], 2, T), bcast(full[:, :], 1, E),
                                             ALU.is_gt))
                tally.settle()
                tally.mark(dve.tensor_reduce(need[:, :], cmp[:, :, :], AX.X, ALU.add))
                tally.mark(dve.tensor_tensor(tiles_before[:, :, :], tiles_before[:, :, :], per_tile[:, :, :],
                                             ALU.subtract))
                tally.settle()
                tally.mark(dve.tensor_tensor_scan(ends[:, :], keep_e[:, :], need[:, :], 0.0, ALU.mult, ALU.add))
                tally.settle()
                tally.mark(dve.tensor_tensor(first[:, :], ends[:, :], need[:, :], ALU.subtract))
                tally.mark(dve.tensor_tensor(past[:, :, :], bcast(tile_no[:, :], 2, E), bcast(ends[:, :], 1, SLOTS),
                                             ALU.is_ge))
                tally.settle()
                tally.mark(dve.tensor_scalar(first[:, :], first[:, :], float(P), None, ALU.mult))
                tally.mark(dve.tensor_reduce(tile_f[:, :], past[:, :, :], AX.X, ALU.add))
                tally.settle()
                tally.mark(dve.tensor_scalar(tile_at[:, :], tile_f[:, :], float(E - 1), None, ALU.min))
                tally.mark(dve.tensor_tensor(where[:, :, :], rank_bank.rearrange("p (t e) -> p t e", e=E),
                                             tiles_before[:, :, :].rearrange("p e t -> p t e"), ALU.add))
                tally.settle()
                tally.mark(dve.tensor_tensor(where[:, :, :], where[:, :, :], bcast(first[:, :], 1, T), ALU.add))
                tally.settle()
                for k in range(2):
                    tally.mark(dve.tensor_tensor(picked[:, k, :, :], hot[:, k, :, :], where[:, :, :], ALU.mult))
                tally.settle()
                tally.mark(dve.tensor_reduce(slot_f[:, :, :], picked[:, :, :, :], AX.X, ALU.add))
                tally.settle()
                tally.mark(dve.tensor_copy(slot[:, :, :], slot_f[:, :, :]))
                tally.settle()


def deal_rows(nc, sem, xn_rows, slot_rows, slot):
    with ExitStack() as ctx:
        xn = ctx.enter_context(nc.sbuf_tensor("xn_all", [P, T, D], F32))
        with nc.Block() as block:
            @block.sync
            def _(sp):
                sp.dma_start(xn[:, :, :], xn_rows.rearrange("(t p) d -> p t d", p=P)).then_inc(sem("xn_back"), 16)

            @block.gpsimd
            def _(pool):
                pool.wait_ge(sem("xn_back"), 16)
                for t in range(T):
                    for k in range(2):
                        pool.indirect_dma_start(
                            out=slot_rows, out_offset=bass.IndirectOffsetOnAxis(ap=slot[:, k, t:t + 1].bitcast(U32), axis=0),
                            in_=xn[:, t, :], in_offset=None).then_inc(sem("dealt"), 16)
                pool.wait_ge(sem("dealt"), 16 * 2 * T)


def run_experts(nc, io, sem, banks, ident, w_up, w_down, tile_at, slot_rows, expert_rows):
    with ExitStack() as ctx:
        def sb(name, shape, dt=F32):
            return ctx.enter_context(nc.sbuf_tensor(name, shape, dt))

        rows = [sb(f"rows{p}", [P, D]) for p in range(2)]
        rowsT = [sb(f"rowsT{p}", [P, DC, P]) for p in range(2)]
        silu = [sb(f"silu{p}", [P, HID]) for p in range(2)]
        hT = [sb(f"hT{p}", [P, HIDC, P]) for p in range(2)]
        res = [sb(f"res{p}", [P, D]) for p in range(2)]
        UP = [banks[:, 3 * p:3 * p + 3, :].rearrange("p b n -> p (b n)")[:, 0:2 * HID] for p in range(2)]
        XT = [banks[:, 3 * p, 0:D] for p in range(2)]
        HT = banks[:, 6:8, :].rearrange("p b n -> p (b n)")[:, 0:HIDC * P]
        Y = banks[:, 6, 0:D]
        cuts = [(n, min(n + 512, 2 * HID)) for n in range(0, 2 * HID, 512)]

        def steps(eng, step):
            with eng.Fori(0, SLOTS // 2 - 1) as turn:
                for p in range(2):
                    step(turn * 2 + p, p, turn, True, True)
            for j in range(SLOTS // 2 * 2 - 2, SLOTS):
                step(j, j % 2, j // 2, j + 1 < SLOTS, j + 2 < SLOTS)

        with nc.Block() as block:
            @block.sync
            def _(sp):
                def load(j, p, turn):
                    sp.wait_ge(sem("rowsT_made"), j + 1)
                    sp.dma_start(rows[p][:, :], slot_rows[bass.ds(j * P, P), :]).then_inc(sem(f"rows{p}"), 16)
                with sp.Fori(0, SLOTS // 2) as turn:
                    for p in range(2):
                        load(turn * 2 + p, p, turn)
                if SLOTS % 2:
                    load(SLOTS - 1, 0, SLOTS // 2)

            @block.tensor
            def _(pe):
                def turn_rows(j, p, turn):
                    pe.wait_ge(sem(f"rows{p}"), turn * 16 + 16)
                    transposes(pe, XT[p].rearrange("p (c n) -> p c n", c=DC), rows[p], ident[:, :], DC
                               ).then_inc(sem("rowsT_made"), 1)

                def up(j, p):
                    e = pe.value_load(tile_at[0:1, bass.ds(j, 1)], min_val=0, max_val=E - 1)
                    pe.wait_ge(sem("rowsT_copied"), j + 1)
                    for c in range(DC):
                        w = w_up[:, bass.ds(e * DC + c, 1), :].rearrange("p c n -> p (c n)")
                        for a, b in cuts:
                            ins = pe.matmul(UP[p][:, a:b], rowsT[p][:, c, :], w[:, a:b], start=(c == 0), stop=(c == 1))
                    ins.then_inc(sem("up_made"), 1)

                def step(j, p, turn, up_ahead, rows_ahead):
                    if up_ahead:
                        up(j + 1, 1 - p)
                    pe.wait_ge(sem("h_ready"), j + 1)
                    pe.wait_ge(sem("y_copied"), j + 1)
                    for c in range(HIDC):
                        n = P if c < HIDC - 1 else HLAST
                        ins = pe.transpose(HT[0:n, c * P:(c + 1) * P], silu[p][:, c * P:c * P + n], ident[:, :])
                    ins.then_inc(sem("hT_made"), 1)
                    if rows_ahead:
                        turn_rows(j + 2, p, turn + 1)
                    e = pe.value_load(tile_at[0:1, bass.ds(j, 1)], min_val=0, max_val=E - 1)
                    pe.wait_ge(sem("hT_low"), j + 1)
                    pe.wait_ge(sem("hT_high"), j + 1)
                    for c in range(HIDC):
                        n = P if c < HIDC - 1 else HLAST
                        w = w_down[:, bass.ds(e * HIDC + c, 1), :].rearrange("p c n -> p (c n)")
                        ins = pe.matmul(Y, hT[p][0:n, c, :], w[0:n, :], start=(c == 0), stop=(c == HIDC - 1))
                    ins.then_inc(sem("y_made"), 1)

                starts_free(pe, sem("rowsT_made"), 2)
                turn_rows(0, 0, 0)
                turn_rows(1, 1, 0)
                pe.wait_ge(sem("up"), 16 * E)
                pe.wait_ge(sem("down"), 2 * 16 * E)
                up(0, 0)
                steps(pe, step)

            @block.scalar
            def _(act):
                def copy_rows(j, p):
                    act.wait_ge(sem("rowsT_made"), j + 3)
                    act.copy(rowsT[p][:, :, :].rearrange("p c n -> p (c n)"), XT[p]).then_inc(sem("rowsT_copied"), 1)

                def gate(j, p):
                    act.wait_ge(sem("up_made"), j + 1)
                    act.activation(silu[p][:, :], UP[p][:, HID:2 * HID], ACT.Silu).then_inc(sem("silu"), 1)

                def step(j, p, turn, up_ahead, rows_ahead):
                    if up_ahead:
                        gate(j + 1, 1 - p)
                    act.wait_ge(sem("hT_made"), j + 1)
                    act.copy(hT[p][:, 0:4, :].rearrange("p c n -> p (c n)"), HT[:, 0:4 * P]
                             ).then_inc(sem("hT_low"), 1)
                    if rows_ahead:
                        copy_rows(j + 2, p)
                    act.wait_ge(sem("y_made"), j + 1)
                    act.wait_ge(sem(f"stored{p}"), turn * 16 + 16)
                    act.copy(res[p][:, :], Y).then_inc(sem("y_copied"), 1)
                    act.wait_ge(sem("y_copied"), j + 2)
                    act.dma_start(expert_rows[bass.ds(j * P, P), :], res[p][:, :]).then_inc(sem(f"stored{p}"), 16)

                starts_free(act, sem("y_copied"), 1)
                for p in range(2):
                    starts_free(act, sem(f"stored{p}"), 16)
                copy_rows(0, 0)
                copy_rows(1, 1)
                gate(0, 0)
                steps(act, step)
                for p in range(2):
                    act.wait_ge(sem(f"stored{p}"), 16 * ((SLOTS + 1 - p) // 2) + 16)

            @block.vector
            def _(dve):
                def hidden(j, p):
                    dve.wait_ge(sem("silu"), j + 1)
                    dve.tensor_tensor(silu[p][:, :], UP[p][:, 0:HID], silu[p][:, :], ALU.mult
                                      ).then_inc(sem("h_ready"), 1)

                def step(j, p, turn, up_ahead, rows_ahead):
                    if up_ahead:
                        hidden(j + 1, 1 - p)
                    dve.wait_ge(sem("hT_made"), j + 1)
                    dve.tensor_copy(hT[p][:, 4:HIDC - 1, :].rearrange("p c n -> p (c n)"),
                                    HT[:, 4 * P:(HIDC - 1) * P]).then_inc(sem("hT_mid"), 1)
                    dve.tensor_copy(hT[p][0:HLAST, HIDC - 1, :], HT[0:HLAST, (HIDC - 1) * P:HIDC * P]
                                    ).then_inc(sem("hT_high"), 1)

                hidden(0, 0)
                steps(dve, step)


def collect_rows(nc, sem, H, minus_half, gate, slot, expert_rows):
    with ExitStack() as ctx:
        def sb(name, shape, dt=F32):
            return ctx.enter_context(nc.sbuf_tensor(name, shape, dt))

        got = [[sb(f"got{p}{k}", [P, D]) for k in range(2)] for p in range(PAIR)]
        s = [dict(r=sb(f"r_c{p}", [P, D])[:, :], stats=sb(f"stats_c{p}", [P, 6])[:, :],
                  agg=sb(f"agg_c{p}", [P, 2])[:, :], pace=sb(f"pace_c{p}", [P, 1])[:, :]) for p in range(PAIR)]
        tiles = range(PAIR)
        with nc.Block() as block:
            @block.gpsimd
            def _(pool):
                for t in range(T):
                    p = t % PAIR
                    if t >= PAIR:
                        pool.wait_ge(sem("added"), t - PAIR + 1)
                    for k in range(2):
                        pool.indirect_dma_start(
                            out=got[p][k][:, :], out_offset=None, in_=expert_rows,
                            in_offset=bass.IndirectOffsetOnAxis(ap=slot[:, k, t:t + 1].bitcast(U32), axis=0)
                        ).then_inc(sem(f"got{p}{k}"), 16)
                    if p == 1 and t >= 3:
                        for q in tiles:
                            rsqrt_pool(pool, sem("ln_var"), t - 3 + q + 1, s[q]["agg"][:, 1:2], minus_half[:, 0:1],
                                       sem("ln_rstd"))
                for q in tiles:
                    rsqrt_pool(pool, sem("ln_var"), T - 1 + q, s[q]["agg"][:, 1:2], minus_half[:, 0:1],
                               sem("ln_rstd"))

            @block.vector
            def _(dve):
                tally = Tally(dve, sem("dve_collect"))
                for turn in range(TURNS):
                    for k in range(2):
                        for p in tiles:
                            t = turn * 2 + p
                            dve.wait_ge(sem(f"got{p}{k}"), 16 * (turn + 1))
                            tally.mark(dve.scalar_tensor_tensor(
                                out=s[p]["r"], in0=got[p][k][:, :], scalar=gate[:, k, t:t + 1],
                                in1=(H[:, t, :], s[p]["r"])[k], op0=ALU.mult, op1=ALU.add))
                        tally.settle()
                    for p in tiles:
                        t = turn * 2 + p
                        dve.tensor_tensor(s[p]["r"], s[p]["r"], H[:, t, :], ALU.add).then_inc(sem("added"), 1)
                    dve.wait_ge(sem("added"), turn * 2 + 2)
                    layer_norm(dve, sem, turn, tally, s, 1e-5, [H[:, turn * 2 + p, :] for p in tiles])
                    dve.wait_ge(sem("ln_done"), turn * 2 + 2)


def vit_rest(nc, io, B, banks, H, ident, ident_bf, minus_half):
    chains = {n: nc.dram_tensor(f"chains_{n}", (CG, P, HD * TOK), F32).ap() for n in "qkvo"}
    rates = nc.dram_tensor("rates", (CG, 2, IMAGES // CG, HEADS, TOK), F32).ap()
    delta_projections(nc, io, banks, H, ident, chains, rates)
    delta_rule(nc, chains, rates)
    inter = nc.dram_tensor("inter", (T * GPT, ME, D), F32).ap()
    with ExitStack() as ctx:
        perm_t = ctx.enter_context(nc.sbuf_tensor("perm_t", [P, T, P], F32))
        with ExitStack() as inner:
            sel = inner.enter_context(nc.sbuf_tensor("sel", [P, DC, ME, T * GPT], F32))
            middle_layers(nc, io, B, H, ident, ident_bf, minus_half, chains["o"], perm_t, sel)
            mixed_experts(nc, io, banks, sel, inter)
        biggest = ctx.enter_context(nc.sbuf_tensor("biggest", [P, 2, T], F32))
        mix_back_and_scan(nc, io, B, H, ident, minus_half, inter, perm_t, biggest)
        int8_layer(nc, io, B, H, ident_bf, minus_half, biggest)



def delta_projections(nc, io, banks, H, ident, chains, rates):
    with ExitStack() as ctx:
        def sb(name, shape, dt=F32):
            return ctx.enter_context(nc.sbuf_tensor(name, shape, dt))

        sem = Sems(nc, ctx, "p")
        N = IMAGES // CG * TOK
        NT = N // P
        w = sb("w_delta", [P, DC, 3 * D])
        w_rate = sb("w_rate", [P, DC, 2 * HEADS])
        x = sb("x_p", [P, NT, D])
        xT = sb("xT_p", [P, DC, N])
        sig = [sb(f"sig{m}", [P, N]) for m in range(2)]
        made = [sb(f"made{m}", [P, N]) for m in range(6)]
        rate = sb("rate_p", [2 * HEADS, N])
        outs = [chains[n].rearrange("g (b h) (d t) -> g h d b t", h=HEADS, d=HD) for n in "qkv"]

        with nc.Block() as block:
            @block.sync
            def _(sp):
                sp.dma_start(w[:, :, :], io["delta_w"]).then_inc(sem("weights"), 16)
                sp.dma_start(w_rate[:, :, :], io["rate_w"]).then_inc(sem("weights"), 16)
                for m in range(6):
                    starts_free(sp, sem(f"stored{m}"), 128)
                starts_free(sp, sem("rate_stored"), 32)
                with sp.Fori(0, CG) as g:
                    for m in range(6):
                        sp.wait_ge(sem(f"made{m}"), g + 2)
                        half = m % 2
                        for b in range(IMAGES // CG):
                            dst = outs[m // 2][bass.ds(g, 1), half * 8:half * 8 + 8, :, b, :].rearrange(
                                "g h d t -> (g h d) t")
                            sp.dma_start(dst, made[m][:, b * TOK:(b + 1) * TOK]).then_inc(sem(f"stored{m}"), 16)
                    sp.wait_ge(sem("rate_made"), g + 2)
                    for kind in range(2):
                        sp.dma_start(rates[bass.ds(g, 1), kind, :, :, :].rearrange("g b h t -> (g h) b t"),
                                     rate[kind * HEADS:(kind + 1) * HEADS, :].rearrange("h (b t) -> h b t", t=TOK)
                                     ).then_inc(sem("rate_stored"), 16)
                for m in range(6):
                    sp.wait_ge(sem(f"stored{m}"), (CG + 1) * 128)
                sp.wait_ge(sem("rate_stored"), (CG + 1) * 32)

            @block.tensor
            def _(pe):
                starts_free(pe, sem("xT_made"), 1)
                pe.wait_ge(sem("weights"), 32)
                with pe.Fori(0, CG) as g:
                    pe.wait_ge(sem("rate_made"), g + 1)
                    pe.wait_ge(sem("x_copied"), g + 1)
                    for i in range(NT):
                        for c in range(DC):
                            ins = pe.transpose(banks[:, c, i * P:(i + 1) * P], x[:, i, c * P:(c + 1) * P], ident[:, :])
                    ins.then_inc(sem("xT_made"), 1)
                    pe.wait_ge(sem("xT_copied"), g + 1)
                    for m in range(6):
                        pe.wait_ge(sem(f"made{m}"), g + 1)
                        for c in range(DC):
                            ins = pe.matmul(banks[:, 2 + m, :], w[:, c, m * P:(m + 1) * P], xT[:, c, :],
                                            start=(c == 0), stop=(c == 1))
                        ins.then_inc(sem("qkv_made"), 1)
                    for c in range(DC):
                        ins = pe.matmul(banks[0:2 * HEADS, 0, :], w_rate[:, c, :], xT[:, c, :], start=(c == 0),
                                        stop=(c == 1))
                    ins.then_inc(sem("rate_logits"), 1)

            @block.scalar
            def _(act):
                starts_free(act, sem("rate_made"), 1)
                for m in range(4, 6):
                    starts_free(act, sem(f"made{m}"), 1)
                with act.Fori(0, CG) as g:
                    act.wait_ge(sem("xT_made"), g + 2)
                    act.copy(xT[:, :, :], banks[:, 0:2, :]).then_inc(sem("xT_copied"), 1)
                    for m in range(4):
                        act.wait_ge(sem("qkv_made"), g * 6 + m + 1)
                        if m >= 2:
                            act.wait_ge(sem(f"made{m - 2}"), g + 2)
                        act.activation(sig[m % 2][:, :], banks[:, 2 + m, :], ACT.Sigmoid).then_inc(sem("sigmoid"), 1)
                    for m in range(4, 6):
                        act.wait_ge(sem("qkv_made"), g * 6 + m + 1)
                        act.wait_ge(sem(f"stored{m}"), g * 128 + 128)
                        act.copy(made[m][:, :], banks[:, 2 + m, :]).then_inc(sem(f"made{m}"), 1)
                    act.wait_ge(sem("rate_logits"), g + 1)
                    act.wait_ge(sem("rate_stored"), g * 32 + 32)
                    act.activation(rate[:, :], banks[0:2 * HEADS, 0, :], ACT.Sigmoid).then_inc(sem("rate_made"), 1)

            @block.vector
            def _(dve):
                for m in range(4):
                    starts_free(dve, sem(f"made{m}"), 1)
                with dve.Fori(0, CG) as g:
                    dve.wait_ge(sem("xT_made"), g + 1)
                    dve.tensor_scalar(x[:, :, :], H[:, bass.ds(g * NT, NT), :], 1.0, None, ALU.mult).then_inc(sem("x_copied"), 1)
                    for m in range(4):
                        dve.wait_ge(sem("sigmoid"), g * 4 + m + 1)
                        dve.wait_ge(sem(f"stored{m}"), g * 128 + 128)
                        dve.tensor_tensor(made[m][:, :], banks[:, 2 + m, :], sig[m % 2][:, :], ALU.mult
                                          ).then_inc(sem(f"made{m}"), 1)


def rsqrt_refined(act, dve, sem, tally, x, y, z, name, value):
    if act is not None:
        act.wait_ge(sem(name + "_x"), value)
        act.activation(y, x, ACT.Sqrt).then_inc(sem(name + "_root"), 1)
        return
    dve.wait_ge(sem(name + "_root"), value)
    tally.mark(dve.reciprocal(y, y))
    tally.settle()
    tally.mark(dve.tensor_tensor(z, y, y, ALU.mult))
    tally.settle()
    tally.mark(dve.tensor_tensor(z, z, x, ALU.mult))
    tally.settle()
    tally.mark(dve.tensor_scalar(z, z, -0.5, 1.5, ALU.mult, ALU.add))
    tally.settle()
    tally.mark(dve.tensor_tensor(y, y, z, ALU.mult))
    tally.settle()


def delta_rule(nc, chains, rates):
    with ExitStack() as ctx:
        def sb(name, shape, dt=F32):
            return ctx.enter_context(nc.sbuf_tensor(name, shape, dt))

        sem = Sems(nc, ctx, "d")
        q, k, v, o = (sb(f"chain_{n}", [P, CG, HD, TOK]) for n in "qkvo")
        ka = sb("ka", [P, CG, HD, TOK])
        rate = sb("rate", [P, CG, 2, TOK])
        n2 = sb("n2", [P, CG, TOK])
        rn = sb("rn", [P, CG, TOK])
        tmp = sb("rn_tmp", [P, CG, TOK])
        f = sb("f", [P, 2, CG, TOK])
        S = [sb(f"S{i}", [P, CG, HD, HD]) for i in range(2)]
        faded = sb("faded", [P, CG, HD, HD])
        prod = sb("prod", [P, CG, HD, HD])
        outer = sb("outer", [P, CG, HD, HD])
        read = sb("read", [P, CG, HD])
        u = sb("u", [P, CG, HD])
        qs = sb("qs", [P, CG, HD, HD])
        flat = "p g d t -> p (g d t)"

        with nc.Block() as block:
            @block.sync
            def _(sp):
                for dst, n in ((k, "k"), (v, "v"), (q, "q")):
                    sp.dma_start(dst[:, :, :, :].rearrange("p g d t -> p g (d t)"),
                                 chains[n].rearrange("g p n -> p g n")).then_inc(sem("loaded_" + n), 16)
                for kind in range(2):
                    for g in range(CG):
                        sp.dma_start(rate[:, g, kind, :], rates[g, kind, :, :, :].rearrange("b h t -> (b h) t")
                                     ).then_inc(sem("loaded_rates"), 16)
                sp.wait_ge(sem("normed_o"), 1)
                sp.dma_start(chains["o"].rearrange("g p n -> p g n"), o[:, :, :, :].rearrange("p g d t -> p g (d t)")
                             ).then_inc(sem("stored"), 16)
                sp.wait_ge(sem("stored"), 16)
                sp.wait_ge(sem("loaded_v"), 16)

            @block.scalar
            def _(act):
                act.wait_ge(sem("loaded_k"), 16)
                act.square(ka[:, :, :, :].rearrange(flat), k[:, :, :, :].rearrange(flat)).then_inc(sem("k_squared"), 1)
                rsqrt_refined(act, None, sem, None, n2[:, :, :], rn[:, :, :], None, "kn", 1)
                act.wait_ge(sem("state"), 1)
                act.wait_ge(sem("loaded_rates"), 16 * 2 * CG)
                with act.Fori(0, TOK // 2) as turn:
                    for i in range(2):
                        act.wait_ge(sem("state"), turn * 2 + i + 1)
                        for g in range(CG):
                            ins = act.activation(faded[:, g, :, :].rearrange("p v k -> p (v k)"),
                                                 S[i][:, g, :, :].rearrange("p v k -> p (v k)"), ACT.Copy,
                                                 scale=rate[:, g, 1, bass.ds(turn * 2 + i, 1)])
                        ins.then_inc(sem("faded"), 1)
                act.wait_ge(sem("o_made"), TOK + 2)
                act.square(q[:, :, :, :].rearrange(flat), o[:, :, :, :].rearrange(flat)).then_inc(sem("o_squared"), 1)
                rsqrt_refined(act, None, sem, None, n2[:, :, :], rn[:, :, :], None, "on", 1)

            @block.vector
            def _(dve):
                once = Tally(dve, sem("dve_once"))
                dve.memset(S[0][:, :, :, :], 0.0).then_inc(sem("state"), 1)
                dve.wait_ge(sem("k_squared"), 1)
                once.mark(dve.tensor_reduce(n2[:, :, :], ka[:, :, :, :].rearrange("p g d t -> p g t d"), AX.X, ALU.add))
                once.settle()
                dve.tensor_scalar(n2[:, :, :], n2[:, :, :], 1e-12, None, ALU.add).then_inc(sem("kn_x"), 1)
                rsqrt_refined(None, dve, sem, once, n2[:, :, :], rn[:, :, :], tmp[:, :, :], "kn", 1)
                dve.wait_ge(sem("loaded_rates"), 16 * 2 * CG)
                once.mark(dve.tensor_tensor(f[:, 0, :, :], rn[:, :, :], rate[:, :, 1, :], ALU.mult))
                once.mark(dve.scalar_tensor_tensor(out=f[:, 1, :, :], in0=rate[:, :, 0, :], scalar=2.0, in1=rn[:, :, :],
                                                   op0=ALU.mult, op1=ALU.mult))
                once.settle()
                once.mark(dve.tensor_tensor(ka[:, :, :, :], k[:, :, :, :], bcast(f[:, 0, :, :], 2, HD), ALU.mult))
                once.settle()
                once.mark(dve.tensor_tensor(k[:, :, :, :], k[:, :, :, :], bcast(f[:, 1, :, :], 2, HD), ALU.mult))
                once.settle()
                dve.wait_ge(sem("loaded_v"), 16)
                with dve.Fori(0, TOK // 2) as turn:
                    tally = Tally(dve, sem("dve_step"), turn, 8)
                    for i in range(2):
                        t = turn * 2 + i
                        now = bass.ds(t, 1)
                        dve.wait_ge(sem("state"), t + 1)
                        tally.mark(dve.tensor_tensor(prod[:, :, :, :], S[i][:, :, :, :],
                                                     bcast(ka[:, :, :, now].rearrange("p g d o -> p g (d o)"), 2, HD),
                                                     ALU.mult))
                        tally.settle()
                        tally.mark(dve.tensor_reduce(read[:, :, :], prod[:, :, :, :], AX.X, ALU.add))
                        tally.settle()
                        tally.mark(dve.tensor_tensor(u[:, :, :], v[:, :, :, now].rearrange("p g d o -> p g (d o)"),
                                                     read[:, :, :], ALU.subtract))
                        tally.settle()
                        tally.mark(dve.tensor_tensor(outer[:, :, :, :],
                                                     bcast(k[:, :, :, now].rearrange("p g d o -> p g (d o)"), 2, HD),
                                                     bcast(u[:, :, :], 3, HD), ALU.mult))
                        tally.settle()
                        dve.wait_ge(sem("faded"), t + 1)
                        dve.wait_ge(sem("o_made"), t + 1)
                        dve.tensor_tensor(S[1 - i][:, :, :, :], faded[:, :, :, :], outer[:, :, :, :], ALU.add
                                          ).then_inc(sem("state"), 1)
                    assert tally.n == 8
                dve.wait_ge(sem("o_squared"), 1)
                once.mark(dve.tensor_reduce(n2[:, :, :], q[:, :, :, :].rearrange("p g d t -> p g t d"), AX.X, ALU.add))
                once.settle()
                dve.tensor_scalar(n2[:, :, :], n2[:, :, :], 1.0 / HD, 1e-6, ALU.mult, ALU.add).then_inc(sem("on_x"), 1)
                rsqrt_refined(None, dve, sem, once, n2[:, :, :], rn[:, :, :], tmp[:, :, :], "on", 1)
                dve.tensor_tensor(o[:, :, :, :], o[:, :, :, :], bcast(rn[:, :, :], 2, HD), ALU.mult
                                  ).then_inc(sem("normed_o"), 1)

            @block.gpsimd
            def _(pool):
                starts_free(pool, sem("o_made"), 2)
                pool.wait_ge(sem("loaded_q"), 16)
                with pool.Fori(0, TOK // 2) as turn:
                    tally = Tally(pool, sem("pool_step"), turn, 8)
                    for i in range(2):
                        t = turn * 2 + i
                        pool.wait_ge(sem("state"), t + 2)
                        now = bass.ds(t, 1)
                        tally.mark(pool.tensor_tensor(qs[:, :, :, :], S[1 - i][:, :, :, :],
                                                      bcast(q[:, :, :, now].rearrange("p g d o -> p g (d o)"), 2, HD),
                                                      ALU.mult))
                        tally.settle()
                        for n in (8, 4, 2):
                            tally.mark(pool.tensor_tensor(qs[:, :, :, 0:n], qs[:, :, :, 0:n], qs[:, :, :, n:2 * n],
                                                          ALU.add))
                            tally.settle()
                        pool.tensor_tensor(o[:, :, :, now].rearrange("p g d o -> p g (d o)"), qs[:, :, :, 0],
                                           qs[:, :, :, 1], ALU.add).then_inc(sem("o_made"), 1)
                        pool.wait_ge(sem("o_made"), t + 3)
                    assert tally.n == 8



def middle_layers(nc, io, B, H, ident, ident_bf, minus_half, o_chains, perm_t, sel):
    with ExitStack() as ctx:
        def sb(name, shape, dt=F32):
            return ctx.enter_context(nc.sbuf_tensor(name, shape, dt))

        sem = Sems(nc, ctx, "b")
        w_o = sb("w_o", [P, DC, D])
        o_norm = sb("o_norm", [P, DC])
        w_r, w_k, w_v = (sb(f"w_{n}", [P, DC, D]) for n in ("mix_r", "mix_k", "mix_v"))
        mu = sb("mu", [P, 2, DC])
        omu = sb("omu", [P, 2, DC])
        w_qkv = sb("w_qkv2", [P, DC, 3 * D])
        w_out = sb("w_out2", [P, DC, D])
        mask = sb("mask_c", [P, HC * P], BF16)
        mask_t = sb("mask_ct", [P, HC * P], BF16)
        control = sb("control", [P, DC, P])
        tie = sb("tie", [P, P])
        in_group = sb("in_group", [P, GPT])
        s = [attention_buffers(nc, ctx, f"b{p}") for p in range(PAIR)]
        oT = [sb(f"o_chain{p}", [P, DC, P]) for p in range(PAIR)]
        mixed = [sb(f"mixed{p}", [P, 2, DC, P]) for p in range(PAIR)]
        gate = [sb(f"gate_b{p}", [P, D]) for p in range(PAIR)]
        kr = [sb(f"kr{p}", [P, DC, P]) for p in range(PAIR)]
        logits = [sb(f"logits{p}", [P, P]) for p in range(PAIR)]
        best = [sb(f"best{p}", [P, GPT]) for p in range(PAIR)]
        perm = [sb(f"perm{p}", [P, P]) for p in range(PAIR)]
        spread = [sb(f"spread{p}", [P, GPT, ME]) for p in range(PAIR)]
        weights = [(w_o, "delta_o_w"), (o_norm, "delta_norm_w"), (w_r, "mix_r_w"), (w_k, "mix_k_w"), (w_v, "mix_v_w"),
                   (mu, "mix_mu"), (w_qkv, "qkv2_w"), (w_out, "out2_w"), (mask, "mask_causal"),
                   (mask_t, "mask_causal_t"), (control, "control"), (tie, "tie"), (in_group, "in_group")]
        tiles = range(PAIR)
        images = o_chains.rearrange("g (b c h) (d t) -> (g b) c (h d) t", c=DC, h=HEADS // DC, d=HD)

        def turned(pe, name, x, bank):
            transposes(pe, bank[:, 0:D].rearrange("p (c n) -> p c n", c=DC), x, ident[:, :], DC
                       ).then_inc(sem(name + "_made"), 1)

        def copied(act, turn, p, name, dst, bank):
            act.wait_ge(sem(name + "_made"), turn * 2 + p + 1)
            act.copy(dst.rearrange("p c n -> p (c n)"), bank[:, 0:D]).then_inc(sem(name + "_copied"), 1)

        with nc.Block() as block:
            @block.sync
            def _(sp):
                for dst, name in weights:
                    sp.dma_start(dst[:], io[name]).then_inc(sem("weights"), 16)
                with sp.Fori(0, TURNS) as turn:
                    for p in tiles:
                        sp.wait_ge(sem("o_used"), turn * 2 + 2)
                        for i in range(2):
                            sp.dma_start(oT[p][:, :, i * TOK:(i + 1) * TOK],
                                         images[bass.ds((turn * 2 + p) * 2 + i, 1), :, :, :]
                                         .rearrange("i c f t -> f (i c) t")).then_inc(sem(f"o_in{p}"), 16)

            @block.gpsimd
            def _(pool):
                with pool.Fori(0, TURNS) as turn:
                    for name in ("ln1", "ln2", "ln3"):
                        for p in tiles:
                            rsqrt_pool(pool, sem(name + "_var"), turn * 2 + p + 1, s[p]["agg"][:, 1:2],
                                       minus_half[:, 0:1], sem(name + "_rstd"))

            @block.tensor
            def _(pe):
                pe.wait_ge(sem("weights"), 16 * len(weights))
                pe.wait_ge(sem("w_o_scaled"), 1)
                starts_free(pe, sem("selected"), 2)
                starts_free(pe, sem("o_used"), 2)
                with pe.Fori(0, TURNS) as turn:
                    pe.wait_ge(sem("sel_stored"), turn * 2 + 2)
                    for p in tiles:
                        pe.wait_ge(sem(f"o_in{p}"), turn * 32 + 32)
                        for c in range(DC):
                            ins = pe.matmul(B[p][0][:, 0:D], oT[p][:, c, :], w_o[:, c, :], start=(c == 0), stop=(c == 1))
                        ins.then_inc(sem("o_used"), 1)
                    for p in tiles:
                        pe.wait_ge(sem("ln1_done"), turn * 2 + p + 1)
                        turned(pe, "x1T", s[p]["x"], B[p][1])
                    for p in tiles:
                        v = turn * 2 + p + 1
                        pe.wait_ge(sem("mixed"), v)
                        for c in range(DC):
                            pe.matmul(B[p][0][:, 0:D], mixed[p][:, 0, c, :], w_r[:, c, :], start=(c == 0), stop=(c == 1))
                        for m in range(DC):
                            for c in range(DC):
                                ins = pe.matmul(B[p][2][:, m * P:(m + 1) * P], w_k[:, c, m * P:(m + 1) * P],
                                                mixed[p][:, 1, c, :], start=(c == 0), stop=(c == 1))
                        ins.then_inc(sem("rk_made"), 1)
                    for p in tiles:
                        v = turn * 2 + p + 1
                        pe.wait_ge(sem("k_act"), v)
                        for c in range(DC):
                            ins = pe.matmul(B[p][3][:, 0:D], kr[p][:, c, :], w_v[:, c, :], start=(c == 0), stop=(c == 1))
                        ins.then_inc(sem("kv_made"), 1)
                    for p in tiles:
                        pe.wait_ge(sem("ln2_done"), turn * 2 + p + 1)
                        turned(pe, "x2T", s[p]["x"], B[p][1])
                    for p in tiles:
                        v = turn * 2 + p + 1
                        pe.wait_ge(sem("x2T_copied"), v)
                        for c in range(DC):
                            pe.matmul(B[p][0], s[p]["xT"][:, c, :], w_qkv[:, c, 0:2 * D], start=(c == 0), stop=(c == 1))
                        for c in range(DC):
                            ins = pe.matmul(B[p][1][:, 0:D], s[p]["xT"][:, c, :], w_qkv[:, c, 2 * D:3 * D],
                                            start=(c == 0), stop=(c == 1))
                        ins.then_inc(sem("qkv_made"), 1)
                    for stage in ("scores", "scores_a", "scores_b", "again", "shifted_a", "shifted_b", "pv",
                                  "turn_back", "o_features"):
                        for p in tiles:
                            attention_pe(pe, sem, turn, p, s[p], B[p], ident[:, :], ident_bf[:, :], mask[:, :],
                                         mask_t[:, :], stage)
                    for p in tiles:
                        v = turn * 2 + p + 1
                        pe.wait_ge(sem("of_copied"), v)
                        for c in range(DC):
                            ins = pe.matmul(B[p][3][:, 0:D], s[p]["of"][:, c, :], w_out[:, c, :], start=(c == 0),
                                            stop=(c == 1))
                        ins.then_inc(sem("projected"), 1)
                    for p in tiles:
                        pe.wait_ge(sem("ln3_done"), turn * 2 + p + 1)
                        turned(pe, "x3T", s[p]["x"], B[p][0])
                    for p in tiles:
                        v = turn * 2 + p + 1
                        pe.wait_ge(sem("x3T_copied"), v)
                        for c in range(DC):
                            ins = pe.matmul(B[p][1][:, 0:P], control[:, c, :], s[p]["xT"][:, c, :], start=(c == 0),
                                            stop=(c == 1))
                        ins.then_inc(sem("logits_made"), 1)
                    for p in tiles:
                        v = turn * 2 + p + 1
                        pe.wait_ge(sem("perm"), v)
                        pe.transpose(B[p][2][:, 0:P], perm[p][:, :], ident[:, :]).then_inc(sem("perm_turned"), 1)
                    for p in tiles:
                        v = turn * 2 + p + 1
                        pe.wait_ge(sem("spread"), v)
                        for c in range(DC):
                            ins = pe.matmul(B[p][(0, 3)[c]], s[p]["x"][:, c * P:(c + 1) * P],
                                            spread[p][:, :, :].rearrange("p g e -> p (g e)"), start=True, stop=True)
                        ins.then_inc(sem("selected"), 1)

            @block.scalar
            def _(act):
                starts_free(act, sem("sel_stored"), 2)
                with act.Fori(0, TURNS) as turn:
                    for p in tiles:
                        copied(act, turn, p, "x1T", s[p]["xT"], B[p][1])
                    for p in tiles:
                        v = turn * 2 + p + 1
                        act.wait_ge(sem("rk_made"), v)
                        act.activation(kr[p][:, :, :].rearrange("p c n -> p (c n)"), B[p][2][:, 0:D], ACT.Relu
                                       ).then_inc(sem("k_relu"), 1)
                        act.activation(gate[p][:, :], B[p][0][:, 0:D], ACT.Sigmoid).then_inc(sem("r_gate"), 1)
                    for p in tiles:
                        copied(act, turn, p, "x2T", s[p]["xT"], B[p][1])
                    for p in tiles:
                        v = turn * 2 + p + 1
                        act.wait_ge(sem("ln2_done"), v)
                        act.wait_ge(sem("qkv_made"), v)
                        for name, bank, at in (("k", 0, D), ("q", 0, 0), ("v", 1, 0)):
                            act.copy(heads(s[p][name + "_ext"])[:, :, 0:HD],
                                     B[p][bank][:, at:at + D].rearrange("p (h x) -> p h x", x=HD)
                                     ).then_inc(sem(name + "_slots"), 1)
                    for stage in ("copies", "again", "exp_a", "exp_b", "oT", "of"):
                        for p in tiles:
                            attention_act(act, sem, turn, p, s[p], B[p], stage, HD ** -0.5)
                    for p in tiles:
                        copied(act, turn, p, "x3T", s[p]["xT"], B[p][0])
                    for p in tiles:
                        t = turn * 2 + p
                        act.wait_ge(sem("selected"), t + 3)
                        for c in range(DC):
                            ins = act.copy(sel[:, c, :, bass.ds(t * GPT, GPT)],
                                           B[p][(0, 3)[c]].rearrange("p (g e) -> p e g", e=ME))
                        ins.then_inc(sem("sel_stored"), 1)
                act.wait_ge(sem("sel_stored"), T + 2)

            @block.vector
            def _(dve):
                once = Tally(dve, sem("cleared"))
                clear_slots(dve, s, once)
                dve.wait_ge(sem("weights"), 16 * len(weights))
                once.mark(dve.tensor_scalar(omu[:, :, :], mu[:, :, :], -1.0, 1.0, ALU.mult, ALU.add))
                for c in range(DC):
                    ins = dve.tensor_scalar(w_o[:, c, :], w_o[:, c, :], o_norm[:, c:c + 1], None, ALU.mult)
                ins.then_inc(sem("w_o_scaled"), 1)
                once.settle()
                with dve.Fori(0, TURNS) as turn:
                    tally = Tally(dve, sem("dve"), turn, PER_B)
                    for p in tiles:
                        t = turn * 2 + p
                        dve.wait_ge(sem("o_used"), t + 3)
                        dve.wait_ge(sem("selected"), turn * 2 + 2)
                        tally.mark(dve.tensor_tensor(s[p]["r"], B[p][0][:, 0:D],
                                                     H[:, bass.ds(t, 1), :].rearrange("p t d -> p (t d)"), ALU.add))
                    tally.settle()
                    layer_norm(dve, sem, turn, tally, s, 1e-5, [s[p]["x"] for p in tiles], "ln1")
                    for p in tiles:
                        v = turn * 2 + p + 1
                        dve.wait_ge(sem("x1T_copied"), v)
                        for m in range(2):
                            for c in range(DC):
                                tally.mark(dve.tensor_scalar(mixed[p][:, m, c, :], s[p]["xT"][:, c, :],
                                                             mu[:, m, c:c + 1], None, ALU.mult))
                    tally.settle()
                    for p in tiles:
                        for m in range(2):
                            for c in range(DC):
                                cur = mixed[p][:, m, c, :].rearrange("p (i t) -> p i t", t=TOK)
                                old = s[p]["xT"][:, c, :].rearrange("p (i t) -> p i t", t=TOK)
                                ins = dve.scalar_tensor_tensor(out=cur[:, :, 1:TOK], in0=old[:, :, 0:TOK - 1],
                                                               scalar=omu[:, m, c:c + 1], in1=cur[:, :, 1:TOK],
                                                               op0=ALU.mult, op1=ALU.add)
                        ins.then_inc(sem("mixed"), 1)
                    for p in tiles:
                        v = turn * 2 + p + 1
                        dve.wait_ge(sem("k_relu"), v)
                        dve.tensor_tensor(kr[p][:, :, :], kr[p][:, :, :], kr[p][:, :, :], ALU.mult
                                          ).then_inc(sem("k_act"), 1)
                    for p in tiles:
                        v = turn * 2 + p + 1
                        dve.wait_ge(sem("kv_made"), v)
                        dve.wait_ge(sem("r_gate"), v)
                        tally.mark(dve.tensor_tensor(s[p]["r"], B[p][3][:, 0:D], gate[p][:, :], ALU.mult))
                    tally.settle()
                    for p in tiles:
                        tally.mark(dve.tensor_tensor(s[p]["r"], s[p]["r"], s[p]["x"], ALU.add))
                    tally.settle()
                    layer_norm(dve, sem, turn, tally, s, 1e-5, [s[p]["x"] for p in tiles], "ln2")
                    for stage in ("max", "divide"):
                        for p in tiles:
                            attention_dve(dve, sem, turn, p, s[p], B[p], tally, stage)
                    for p in tiles:
                        v = turn * 2 + p + 1
                        dve.wait_ge(sem("projected"), v)
                        tally.mark(dve.tensor_tensor(s[p]["r"], B[p][3][:, 0:D], s[p]["x"], ALU.add))
                    tally.settle()
                    layer_norm(dve, sem, turn, tally, s, 1e-5, [s[p]["x"] for p in tiles], "ln3")
                    for p in tiles:
                        t = turn * 2 + p
                        dve.wait_ge(sem("ln3_done"), t + 1)
                        tally.mark(kept(dve, H[:, bass.ds(t, 1), :].rearrange("p t d -> p (t d)"), s[p]["x"]))
                    for p in tiles:
                        v = turn * 2 + p + 1
                        dve.wait_ge(sem("logits_made"), v)
                        tally.mark(dve.tensor_tensor(logits[p][:, :], B[p][1][:, 0:P], tie[:, :], ALU.add))
                    tally.settle()
                    for p in tiles:
                        tally.mark(dve.tensor_reduce(best[p][:, :], logits[p][:, :].rearrange("p (g t) -> p g t", t=GROUP),
                                                     AX.X, ALU.max))
                    tally.settle()
                    for p in tiles:
                        dve.tensor_tensor(perm[p][:, :].rearrange("p (g t) -> p g t", t=GROUP),
                                          logits[p][:, :].rearrange("p (g t) -> p g t", t=GROUP),
                                          bcast(best[p][:, :], 2, GROUP), ALU.is_equal).then_inc(sem("perm"), 1)
                    for p in tiles:
                        t = turn * 2 + p
                        dve.wait_ge(sem("perm"), t + 1)
                        tally.mark(kept(dve, perm_t[:, bass.ds(t, 1), :].rearrange("p t n -> p (t n)"),
                                                   perm[p][:, :]))
                    for p in tiles:
                        v = turn * 2 + p + 1
                        dve.wait_ge(sem("perm_turned"), v)
                        dve.tensor_tensor(spread[p][:, :, :], bcast(B[p][2][:, 0:ME], 1, GPT),
                                          bcast(in_group[:, :], 2, ME), ALU.mult).then_inc(sem("spread"), 1)
                    tally.settle()
                    assert tally.n == PER_B, tally.n


PER_B = 38


def mixed_experts(nc, io, banks, sel, inter):
    QUAD = 4
    with ExitStack() as ctx:
        def sb(name, shape, dt=F32):
            return ctx.enter_context(nc.sbuf_tensor(name, shape, dt))

        sem = Sems(nc, ctx, "x")
        f1 = [sb(f"f1_{p}", [P, DC, FE]) for p in range(QUAD)]
        f2 = [sb(f"f2_{p}", [FE, D]) for p in range(QUAD)]
        bias = sb("bias_x", [FE, ME])
        inner = [sb(f"inner{p}", [FE, T * GPT]) for p in range(QUAD)]
        res = [sb(f"res_x{p}", [P, D]) for p in range(QUAD)]
        tiles = range(QUAD)
        with nc.Block() as block:
            @block.sync
            def _(sp):
                sp.dma_start(bias[:, :], io["mote_bias"]).then_inc(sem("bias"), 16)
                with sp.Fori(0, ME // QUAD) as turn:
                    for p in tiles:
                        sp.wait_ge(sem(f"out_made{p}"), turn + 1)
                        sp.dma_start(f1[p][:, :, :], io["f1"][bass.ds(turn * QUAD + p, 1), :, :, :]
                                     .rearrange("e p c f -> (e p) c f")).then_inc(sem(f"f_in{p}"), 16)
                        sp.dma_start(f2[p][:, :], io["f2"][bass.ds(turn * QUAD + p, 1), :, :]
                                     .rearrange("e f d -> (e f) d")).then_inc(sem(f"f_in{p}"), 16)

            @block.tensor
            def _(pe):
                for p in tiles:
                    starts_free(pe, sem(f"out_made{p}"), 1)
                with pe.Fori(0, ME // QUAD) as turn:
                    for p in tiles:
                        pe.wait_ge(sem(f"f_in{p}"), turn * 32 + 32)
                        pe.wait_ge(sem(f"inner{p}"), turn + 1)
                        for c in range(DC):
                            ins = pe.matmul(banks[0:FE, 2 * p, 0:P], f1[p][:, c, :],
                                            sel[:, c, bass.ds(turn * QUAD + p, 1), :].rearrange("p e g -> p (e g)"),
                                            start=(c == 0), stop=(c == 1))
                        ins.then_inc(sem(f"hidden{p}"), 1)
                    for p in tiles:
                        pe.wait_ge(sem(f"inner{p}"), turn + 2)
                        pe.wait_ge(sem(f"res{p}"), turn + 1)
                        pe.matmul(banks[:, 2 * p + 1, 0:D], inner[p][:, :], f2[p][:, :], start=True, stop=True
                                  ).then_inc(sem(f"out_made{p}"), 1)

            @block.scalar
            def _(act):
                act.wait_ge(sem("bias"), 16)
                for p in tiles:
                    starts_free(act, sem(f"inner{p}"), 1)
                    starts_free(act, sem(f"stored{p}"), 16)
                with act.Fori(0, ME // QUAD) as turn:
                    for p in tiles:
                        act.wait_ge(sem(f"hidden{p}"), turn + 1)
                        act.activation(inner[p][:, :], banks[0:FE, 2 * p, 0:P], ACT.Relu,
                                       bias=bias[:, bass.ds(turn * QUAD + p, 1)]).then_inc(sem(f"inner{p}"), 1)
                    for p in tiles:
                        act.wait_ge(sem(f"res{p}"), turn + 2)
                        act.dma_start(inter[:, bass.ds(turn * QUAD + p, 1), :].rearrange("g e d -> g (e d)"),
                                      res[p][:, :]).then_inc(sem(f"stored{p}"), 16)
                for p in tiles:
                    act.wait_ge(sem(f"stored{p}"), 16 * ME // QUAD + 16)

            @block.vector
            def _(dve):
                for p in tiles:
                    starts_free(dve, sem(f"res{p}"), 1)
                with dve.Fori(0, ME // QUAD) as turn:
                    for p in tiles:
                        dve.wait_ge(sem(f"out_made{p}"), turn + 2)
                        dve.wait_ge(sem(f"stored{p}"), turn * 16 + 16)
                        dve.tensor_copy(res[p][:, :], banks[:, 2 * p + 1, 0:D]).then_inc(sem(f"res{p}"), 1)


def mix_back_and_scan(nc, io, B, H, ident, minus_half, inter, perm_t, biggest):
    with ExitStack() as ctx:
        def sb(name, shape, dt=F32):
            return ctx.enter_context(nc.sbuf_tensor(name, shape, dt))

        sem = Sems(nc, ctx, "e")
        NP = GPT // 2
        own_pair = sb("own_pair", [P, NP, P])
        w_lam = sb("w_lam", [P, DC, D])
        b_lam = sb("b_lam", [P, DC])
        back = [sb(f"back{p}", [P, NP, D]) for p in range(PAIR)]
        to = [sb(f"to{p}", [P, NP, P]) for p in range(PAIR)]
        xT = [sb(f"xT_e{p}", [P, DC, P]) for p in range(PAIR)]
        lam = [sb(f"lam{p}", [P, DC, P]) for p in range(PAIR)]
        ug = [sb(f"ug{p}", [P, DC, P]) for p in range(PAIR)]
        y = [sb(f"y{p}", [P, DC * P]) for p in range(PAIR)]
        s = [dict(r=sb(f"r_e{p}", [P, D])[:, :], x=sb(f"x_e{p}", [P, D])[:, :], stats=sb(f"stats_e{p}", [P, 6])[:, :],
                  agg=sb(f"agg_e{p}", [P, 2])[:, :], pace=sb(f"pace_e{p}", [P, 1])[:, :]) for p in range(PAIR)]
        weights = [(own_pair, "own_pair"), (w_lam, "lam_w"), (b_lam, "lam_b")]
        tiles = range(PAIR)
        with nc.Block() as block:
            @block.sync
            def _(sp):
                for dst, name in weights:
                    sp.dma_start(dst[:], io[name]).then_inc(sem("weights"), 16)
                with sp.Fori(0, TURNS) as turn:
                    for p in tiles:
                        sp.wait_ge(sem("mixed_back"), turn * 2 + 2)
                        for k in range(NP):
                            sp.dma_start(back[p][:, k, :], inter[bass.ds((turn * 2 + p) * GPT + 2 * k, 2), :, :]
                                         .rearrange("g e d -> (g e) d")).then_inc(sem(f"back{p}"), 16)

            @block.gpsimd
            def _(pool):
                with pool.Fori(0, TURNS) as turn:
                    for name in ("ln1", "ln2"):
                        for p in tiles:
                            rsqrt_pool(pool, sem(name + "_var"), turn * 2 + p + 1, s[p]["agg"][:, 1:2],
                                       minus_half[:, 0:1], sem(name + "_rstd"))

            @block.tensor
            def _(pe):
                starts_free(pe, sem("mixed_back"), 2)
                pe.wait_ge(sem("weights"), 16 * len(weights))
                with pe.Fori(0, TURNS) as turn:
                    for p in tiles:
                        pe.wait_ge(sem("to"), turn * 2 + p + 1)
                        pe.wait_ge(sem(f"back{p}"), turn * 16 * NP + 16 * NP)
                        for k in range(NP):
                            ins = pe.matmul(B[p][0][:, 0:D], to[p][:, k, :], back[p][:, k, :], start=(k == 0),
                                            stop=(k == NP - 1))
                        ins.then_inc(sem("mixed_back"), 1)
                    for p in tiles:
                        pe.wait_ge(sem("ln1_done"), turn * 2 + p + 1)
                        transposes(pe, B[p][1][:, 0:D].rearrange("p (c n) -> p c n", c=DC), s[p]["x"], ident[:, :], DC
                                   ).then_inc(sem("xT_made"), 1)
                    for p in tiles:
                        pe.wait_ge(sem("xT_copied"), turn * 2 + p + 1)
                        for m in range(DC):
                            for c in range(DC):
                                ins = pe.matmul(B[p][2][:, m * P:(m + 1) * P], w_lam[:, c, m * P:(m + 1) * P],
                                                xT[p][:, c, :], start=(c == 0), stop=(c == 1))
                        ins.then_inc(sem("lam_logits"), 1)
                    for p in tiles:
                        pe.wait_ge(sem("scanned"), turn * 2 + p + 1)
                        transposes(pe, B[p][3][:, 0:D].rearrange("p (c n) -> p c n", c=DC), y[p], ident[:, :], DC
                                   ).then_inc(sem("y_turned"), 1)

            @block.scalar
            def _(act):
                act.wait_ge(sem("weights"), 16 * len(weights))
                with act.Fori(0, TURNS) as turn:
                    for p in tiles:
                        act.wait_ge(sem("xT_made"), turn * 2 + p + 1)
                        act.copy(xT[p][:, :, :].rearrange("p c n -> p (c n)"), B[p][1][:, 0:D]
                                 ).then_inc(sem("xT_copied"), 1)
                    for p in tiles:
                        act.wait_ge(sem("lam_logits"), turn * 2 + p + 1)
                        for m in range(DC):
                            ins = act.activation(lam[p][:, m, :], B[p][2][:, m * P:(m + 1) * P], ACT.Sigmoid,
                                                 bias=b_lam[:, m:m + 1])
                        ins.then_inc(sem("lam"), 1)

            @block.vector
            def _(dve):
                dve.wait_ge(sem("weights"), 16 * len(weights))
                with dve.Fori(0, TURNS) as turn:
                    tally = Tally(dve, sem("dve"), turn, PER_E)
                    for p in tiles:
                        t = turn * 2 + p
                        dve.tensor_tensor(to[p][:, :, :], bcast(perm_t[:, bass.ds(t, 1), :]
                                                                .rearrange("p t n -> p (t n)"), 1, NP),
                                          own_pair[:, :, :], ALU.mult).then_inc(sem("to"), 1)
                    for p in tiles:
                        t = turn * 2 + p
                        dve.wait_ge(sem("mixed_back"), t + 3)
                        tally.mark(dve.tensor_tensor(s[p]["r"], B[p][0][:, 0:D],
                                                     H[:, bass.ds(t, 1), :].rearrange("p t d -> p (t d)"), ALU.add))
                    tally.settle()
                    layer_norm(dve, sem, turn, tally, s, 1e-5, [s[p]["x"] for p in tiles], "ln1")
                    for p in tiles:
                        v = turn * 2 + p + 1
                        dve.wait_ge(sem("lam"), v)
                        dve.wait_ge(sem("xT_copied"), v)
                        tally.mark(dve.tensor_scalar(ug[p][:, :, :], lam[p][:, :, :], -1.0, 1.0, ALU.mult, ALU.add))
                    tally.settle()
                    for p in tiles:
                        tally.mark(dve.tensor_tensor(ug[p][:, :, :], ug[p][:, :, :], xT[p][:, :, :], ALU.mult))
                        tally.mark(dve.memset(lam[p][:, :, :].rearrange("p c (i t) -> p (c i) t", t=TOK)[:, :, 0], 0.0))
                    tally.settle()
                    for p in tiles:
                        dve.tensor_tensor_scan(y[p][:, :], lam[p][:, :, :].rearrange("p c n -> p (c n)"),
                                               ug[p][:, :, :].rearrange("p c n -> p (c n)"), 0.0, ALU.mult, ALU.add
                                               ).then_inc(sem("scanned"), 1)
                    for p in tiles:
                        dve.wait_ge(sem("y_turned"), turn * 2 + p + 1)
                        tally.mark(dve.tensor_tensor(s[p]["r"], B[p][3][:, 0:D], s[p]["x"], ALU.add))
                    tally.settle()
                    layer_norm(dve, sem, turn, tally, s, 1e-5, [s[p]["x"] for p in tiles], "ln2")
                    for p in tiles:
                        t = turn * 2 + p
                        dve.wait_ge(sem("ln2_done"), t + 1)
                        tally.mark(kept(dve, H[:, bass.ds(t, 1), :].rearrange("p t d -> p (t d)"), s[p]["x"]))
                        tally.mark(dve.tensor_reduce(biggest[:, 0, bass.ds(t, 1)], s[p]["x"], AX.X, ALU.max))
                        tally.mark(dve.tensor_reduce(biggest[:, 1, bass.ds(t, 1)], s[p]["x"], AX.X, ALU.min,
                                                     negate=True))
                    tally.settle()
                    assert tally.n == PER_E, tally.n


PER_E = 24


def int8_layer(nc, io, B, H, ident_bf, minus_half, biggest):
    with ExitStack() as ctx:
        def sb(name, shape, dt=F32):
            return ctx.enter_context(nc.sbuf_tensor(name, shape, dt))

        sem = Sems(nc, ctx, "q")
        w8 = sb("w8", [P, DC, D // 4], I32)
        w = sb("w_int", [P, DC, D], BF16)
        w_scale = sb("w_scale", [P, D])
        bias = sb("bias_q", [P, D])
        top = sb("top_q", [P, 1])
        scale = sb("scale_q", [P, 1])
        inv = sb("inv_q", [P, 1])
        qf = [sb(f"qf{p}", [P, D]) for p in range(PAIR)]
        qb = [sb(f"qb{p}", [P, D], BF16) for p in range(PAIR)]
        qT = [sb(f"qT_q{p}", [P, DC, P], BF16) for p in range(PAIR)]
        res = [sb(f"res_q{p}", [P, D]) for p in range(PAIR)]
        s = [dict(r=sb(f"r_q{p}", [P, D])[:, :], stats=sb(f"stats_q{p}", [P, 6])[:, :],
                  agg=sb(f"agg_q{p}", [P, 2])[:, :], pace=sb(f"pace_q{p}", [P, 1])[:, :]) for p in range(PAIR)]
        weights = [(w8, "int8_w"), (w_scale, "int8_scale"), (bias, "int8_b")]
        tiles = range(PAIR)
        TB = [B[p][0].bitcast(BF16)[:, 0:D] for p in range(PAIR)]
        with nc.Block() as block:
            @block.sync
            def _(sp):
                for dst, name in weights:
                    sp.dma_start(dst[:], io[name]).then_inc(sem("weights"), 16)
                for p in tiles:
                    starts_free(sp, sem(f"out{p}"), 16)
                with sp.Fori(0, TURNS) as turn:
                    for p in tiles:
                        sp.wait_ge(sem("ln_done"), turn * 2 + p + 1)
                        sp.dma_start(io["out"][bass.ds((turn * 2 + p) * P, P), :], res[p][:, :]
                                     ).then_inc(sem(f"out{p}"), 16)
                for p in tiles:
                    sp.wait_ge(sem(f"out{p}"), 16 * TURNS + 16)

            @block.gpsimd
            def _(pool):
                pool.wait_ge(sem("row_max"), 1)
                pool.partition_all_reduce(scale[:, :], top[:, :], P, bass.bass_isa.ReduceOp.max).then_inc(sem("max"), 1)
                with pool.Fori(0, TURNS) as turn:
                    for p in tiles:
                        rsqrt_pool(pool, sem("ln_var"), turn * 2 + p + 1, s[p]["agg"][:, 1:2], minus_half[:, 0:1],
                                   sem("ln_rstd"))

            @block.tensor
            def _(pe):
                pe.wait_ge(sem("w_ready"), 1)
                with pe.Fori(0, TURNS) as turn:
                    for p in tiles:
                        pe.wait_ge(sem("q_ready"), turn * 2 + p + 1)
                        for c in range(DC):
                            ins = pe.transpose(TB[p][:, c * P:(c + 1) * P], qb[p][:, c * P:(c + 1) * P], ident_bf[:, :])
                        ins.then_inc(sem("qT_made"), 1)
                    for p in tiles:
                        pe.wait_ge(sem("qT_copied"), turn * 2 + p + 1)
                        for c in range(DC):
                            ins = pe.matmul(B[p][1][:, 0:D], qT[p][:, c, :], w[:, c, :], start=(c == 0), stop=(c == 1))
                        ins.then_inc(sem("sums"), 1)

            @block.scalar
            def _(act):
                act.wait_ge(sem("weights"), 16 * len(weights))
                act.copy(w[:, :, :], w8[:, :, :].bitcast(I8)).then_inc(sem("w_ready"), 1)
                with act.Fori(0, TURNS) as turn:
                    for p in tiles:
                        act.wait_ge(sem("qT_made"), turn * 2 + p + 1)
                        act.copy(qT[p][:, :, :].rearrange("p c n -> p (c n)"), TB[p]).then_inc(sem("qT_copied"), 1)

            @block.vector
            def _(dve):
                dve.tensor_reduce(top[:, :], biggest[:, :, :], AX.XY, ALU.max).then_inc(sem("row_max"), 1)
                once = Tally(dve, sem("dve_once"))
                dve.wait_ge(sem("max"), 1)
                once.mark(dve.tensor_scalar(scale[:, :], scale[:, :], 1.0 / 127.0, 1e-5, ALU.mult, ALU.max))
                once.settle()
                once.mark(dve.reciprocal(inv[:, :], scale[:, :]))
                once.settle()
                dve.wait_ge(sem("weights"), 16 * len(weights))
                with dve.Fori(0, TURNS) as turn:
                    tally = Tally(dve, sem("dve"), turn, PER_Q)
                    for p in tiles:
                        tally.mark(dve.tensor_scalar(qf[p][:, :], H[:, bass.ds(turn * 2 + p, 1), :]
                                                     .rearrange("p t d -> p (t d)"), inv[:, :], None, ALU.mult))
                    tally.settle()
                    for p in tiles:
                        tally.mark(dve.tensor_scalar(qf[p][:, :], qf[p][:, :], MAGIC, MAGIC, ALU.add, ALU.subtract))
                    tally.settle()
                    for p in tiles:
                        dve.tensor_scalar(qb[p][:, :], qf[p][:, :], 127.0, -128.0, ALU.min, ALU.max
                                          ).then_inc(sem("q_ready"), 1)
                    for p in tiles:
                        dve.wait_ge(sem("sums"), turn * 2 + p + 1)
                        tally.mark(dve.scalar_tensor_tensor(out=s[p]["r"], in0=B[p][1][:, 0:D], scalar=scale[:, 0:1],
                                                            in1=w_scale[:, :], op0=ALU.mult, op1=ALU.mult))
                    tally.settle()
                    for p in tiles:
                        tally.mark(dve.tensor_tensor(s[p]["r"], s[p]["r"], bias[:, :], ALU.add))
                    tally.settle()
                    for p in tiles:
                        tally.mark(dve.tensor_tensor(s[p]["r"], s[p]["r"], H[:, bass.ds(turn * 2 + p, 1), :]
                                                     .rearrange("p t d -> p (t d)"), ALU.add))
                    tally.settle()
                    for p in tiles:
                        dve.wait_ge(sem(f"out{p}"), turn * 16 + 16)
                    layer_norm(dve, sem, turn, tally, s, 1e-5, [res[p][:, :] for p in tiles])
                    dve.wait_ge(sem("ln_done"), turn * 2 + 2)
                    assert tally.n == PER_Q, tally.n


PER_Q = 14


def laid_out_more(inputs, a, rows, wide, tok):
    import numpy as np

    up = a("L0_ffn_w_up").transpose(2, 0, 1).reshape(DC, P, E, 2 * HID).transpose(1, 2, 0, 3)
    down = np.pad(a("L0_ffn_w_down").transpose(2, 0, 1), ((0, HIDC * P - HID), (0, 0), (0, 0)))
    down = down.reshape(HIDC, P, E, D).transpose(1, 2, 0, 3)

    def line(v):
        return np.broadcast_to(np.asarray(v, np.float32)[None, :], (P, len(v)))

    def columns(v):
        return v.reshape(DC, P).T

    control = a("L2_ffn_controller").reshape(D, ME)
    group = tok // GROUP
    pairs = np.arange(GPT // 2)
    own = (group[None, None, :] == 2 * pairs[None, :, None] + (tok // ME)[:, None, None]).astype(np.float32)
    keep = np.tile(np.arange(T) > 0, E)
    return {
        "up_w": up,
        "down_w": down,
        "ramp": line(np.arange(E)),
        "before": (tok[:, None] < tok[None, :]).astype(np.float32),
        "ones": np.ones((P, P), np.float32),
        "keep": line(keep),
        "keep_e": line(np.ones(E)),
        "full": line(P * np.arange(T)),
        "tile_no": line(np.arange(SLOTS)),
        "delta_w": rows(np.concatenate([a("L1_attn_Wq"), a("L1_attn_Wk"), a("L1_attn_Wv")], 1)),
        "rate_w": rows(np.concatenate([a("L1_attn_Wbet"), a("L1_attn_Wf")], 1)),
        "delta_o_w": rows(a("L1_attn_Wo")),
        "delta_norm_w": columns(a("L1_attn_norm_w")),
        "mix_r_w": rows(a("L1_ffn_W_r").T),
        "mix_k_w": rows(a("L1_ffn_W_k").T),
        "mix_v_w": rows(a("L1_ffn_W_v").T),
        "mix_mu": np.stack([columns(a("L1_ffn_mu_r")), columns(a("L1_ffn_mu_k"))], 1),
        "qkv2_w": rows(a("L2_attn_w_qkv").T),
        "out2_w": rows(a("L2_attn_w_out").T),
        "control": rows(np.concatenate([control, control], 1)),
        "tie": line(np.tile(np.linspace(0.0, 1e-6, GROUP, dtype=np.float32), GPT)),
        "in_group": (group[:, None] == np.arange(GPT)[None, :]).astype(np.float32),
        "mote_bias": a("L2_ffn_bias").reshape(ME, FE).T,
        "f1": a("L2_ffn_f1").reshape(DC, P, ME, FE).transpose(2, 1, 0, 3),
        "f2": a("L2_ffn_f2").reshape(ME, FE, D),
        "own_pair": own,
        "lam_w": rows(a("L3_attn_W").T),
        "lam_b": columns(a("L3_attn_b")),
        "int8_w": rows(a("L3_ffn_weight_int8").T).view(np.int32),
        "int8_scale": wide(a("L3_ffn_weight_scale").reshape(-1)),
        "int8_b": wide(a("L3_ffn_bias")),
    }


def laid_out(inputs):
    import numpy as np

    def a(name):
        return np.asarray(inputs[name])

    def rows(w):
        return np.ascontiguousarray(w.reshape(-1, P, w.shape[-1]).transpose(1, 0, 2))

    def wide(v, times=1):
        return np.ascontiguousarray(np.broadcast_to(np.tile(v, times)[None, :], (P, v.size * times)))

    x = a("x").reshape(IMAGES, 3, 8, 16, 8, 16).transpose(1, 3, 5, 0, 2, 4).reshape(PC, P, T, P)
    neg = np.float32(-1e30)
    tok = np.arange(P)
    pair = np.where(tok[:, None] // TOK == tok[None, :] // TOK, 0, neg).astype(np.float32)
    causal = np.where((pair == 0) & (tok[None, :] <= tok[:, None]), 0, neg).astype(np.float32)
    bf = np.dtype("bfloat16")
    r = {
        "ident": np.eye(P, dtype=np.float32),
        "ident_bf": np.eye(P).astype(bf),
        "patches": np.ascontiguousarray(x.transpose(2, 1, 0, 3)),
        "tok_w": rows(a("L0_tok_W").T),
        "tok_b": wide(a("L0_tok_b")),
        "qkv_w": rows(a("L0_attn_qkv_w").T),
        "qk_w": np.concatenate([wide(a("L0_attn_q_norm_w"), HEADS), wide(a("L0_attn_k_norm_w"), HEADS)], 1),
        "qk_b": np.concatenate([wide(a("L0_attn_q_norm_b"), HEADS), wide(a("L0_attn_k_norm_b"), HEADS)], 1),
        "proj_w": rows(a("L0_attn_proj_w").T),
        "proj_b": wide(a("L0_attn_proj_b")),
        "token_mean": (pair == 0).astype(np.float32) / np.float32(TOK),
        "rms_w": wide(a("L0_ffn_norm_scale")),
        "router_w": rows(a("L0_ffn_w_router").T),
        "mask_pair": np.tile(pair, (1, HC)).astype(bf),
        "mask_causal": np.tile(causal, (1, HC)).astype(bf),
        "mask_causal_t": np.tile(causal.T, (1, HC)).astype(bf),
    }
    r.update(laid_out_more(inputs, a, rows, wide, tok))
    return {k: np.ascontiguousarray(v) for k, v in r.items()}


def kernel(**inputs):
    import concourse.bacc as bacc
    from concourse.bass_utils import run_bass_kernel_spmd as launch

    arrays = laid_out(inputs)
    nc = bacc.Bacc("TRN2", target_bir_lowering=False, num_devices=1)
    io = {n: nc.dram_tensor("in_" + n, a.shape, mybir.dt.from_np(a.dtype), kind="ExternalInput").ap()
          for n, a in arrays.items()}
    out = nc.dram_tensor("out", (IMAGES * TOK, D), F32, kind="ExternalOutput").ap()
    vit_tower(nc, io, out)
    r = launch(nc, [{"in_" + n: a for n, a in arrays.items()}], core_ids=[0])
    return r.results[0]["out"].reshape(IMAGES, TOK, D)
```
